# Optimizing a Trainium2 kernel written in Bass

```python
import numpy as np
import jax
import jax.numpy as jnp

def _softmax(x, axis=-1):
    return jax.nn.softmax(x, axis=axis)

def _gelu(x):
    return jax.nn.gelu(x, approximate=True)

def _silu(x):
    return jax.nn.silu(x)

def _sigmoid(x):
    return jax.nn.sigmoid(x)

def _layernorm(x, axis=-1, eps=1e-05):
    m = jnp.mean(x, axis=axis, keepdims=True)
    v = jnp.var(x, axis=axis, keepdims=True)
    return (x - m) / jnp.sqrt(v + eps)

def _scatter_add(tgt, idx, src, axis=0):
    return tgt.at[idx].add(src)

def _segment_sum(src, seg, n):
    return jax.ops.segment_sum(src, seg, n)
kernel_name = 'mk_hybrid_d1_jaxref_r8_73be2f'

def setup_inputs(seed: int=0):
    np.random.seed(seed)
    _w = jnp.asarray

    def _L0_attn_a_setup():
        import jax, jax.numpy as jnp
        import numpy as np
        EMB_DIM = 128
        N_HEADS = 16
        HEAD_DIM = EMB_DIM // N_HEADS
        SEQ = 256
        BSZ = 2

        def _rope_pair(q, k):
            bsz, seq_len, d_model = q.shape
            freq_range = jnp.arange(d_model // 2, dtype=jnp.float32)
            freq_cis = jnp.power(10000.0, -2.0 * freq_range / d_model)
            pos = jnp.arange(seq_len, dtype=jnp.float32)
            freq = jnp.einsum('i,j->ij', pos, freq_cis)
            sin_e = jnp.sin(freq)[None]
            cos_e = jnp.cos(freq)[None]
            q_even, q_odd = (q[..., ::2], q[..., 1::2])
            k_even, k_odd = (k[..., ::2], k[..., 1::2])
            q_rot = jnp.concatenate([q_even * cos_e - q_odd * sin_e, q_even * sin_e - q_odd * cos_e], axis=-1)
            k_rot = jnp.concatenate([k_even * cos_e - k_odd * sin_e, k_even * sin_e - k_odd * cos_e], axis=-1)
            return (q_rot, k_rot)
        key = jax.random.key(seed)
        ks = jax.random.split(key, 9)
        s = 1.0 / np.sqrt(EMB_DIM)
        return {'x': jax.random.normal(ks[0], (BSZ, SEQ, EMB_DIM), dtype=jnp.float32), 'Wq': jax.random.normal(ks[1], (EMB_DIM, EMB_DIM), dtype=jnp.float32) * s, 'bq': jax.random.normal(ks[2], (EMB_DIM,), dtype=jnp.float32) * 0.02, 'Wk': jax.random.normal(ks[3], (EMB_DIM, EMB_DIM), dtype=jnp.float32) * s, 'bk': jax.random.normal(ks[4], (EMB_DIM,), dtype=jnp.float32) * 0.02, 'Wv': jax.random.normal(ks[5], (EMB_DIM, EMB_DIM), dtype=jnp.float32) * s, 'bv': jax.random.normal(ks[6], (EMB_DIM,), dtype=jnp.float32) * 0.02, 'Wo': jax.random.normal(ks[7], (EMB_DIM, EMB_DIM), dtype=jnp.float32) * s, 'bo': jax.random.normal(ks[8], (EMB_DIM,), dtype=jnp.float32) * 0.02}
    _L0_attn_a_in = _L0_attn_a_setup()

    def _L0_attn_b_setup():
        import jax, jax.numpy as jnp
        import numpy as np
        import math
        D_MODEL = 128
        N_HEADS = 16
        D_HEAD = D_MODEL // N_HEADS
        DECAY_MAX = 0.99
        LN_EPS = 1e-05

        def _decay_mask(S):
            i = jnp.arange(S, dtype=jnp.float32)[:, None]
            j = jnp.arange(S, dtype=jnp.float32)[None, :]
            diff = i - j
            return jnp.where(diff >= 0, jnp.power(jnp.float32(DECAY_MAX), diff), 0.0)
        key = jax.random.key(seed)
        ks = jax.random.split(key, 12)
        B, S = (2, 256)
        x = jax.random.normal(ks[0], (B, S, D_MODEL), dtype=jnp.float32)

        def w(k):
            return jax.random.normal(k, (D_MODEL, D_MODEL), dtype=jnp.float32) * 0.02
        return {'x': x, 'Wq': w(ks[1]), 'bq': jnp.zeros((D_MODEL,), jnp.float32), 'Wk': w(ks[2]), 'bk': jnp.zeros((D_MODEL,), jnp.float32), 'Wv': w(ks[3]), 'bv': jnp.zeros((D_MODEL,), jnp.float32), 'Wg': w(ks[4]), 'bg': jnp.zeros((D_MODEL,), jnp.float32), 'Wo': w(ks[5]), 'bo': jnp.zeros((D_MODEL,), jnp.float32), 'gamma': jnp.ones((D_MODEL,), jnp.float32), 'beta': jnp.zeros((D_MODEL,), jnp.float32)}
    _L0_attn_b_in = _L0_attn_b_setup()

    def _L0_ffn_setup():
        import jax, jax.numpy as jnp
        import numpy as np
        DIM = 128

        def _reference_tuple_inner(x, W_r, W_k, W_v, mu_r, mu_k):
            B, T, C = x.shape
            x_prev = jnp.concatenate([jnp.zeros((B, 1, C), x.dtype), x[:, :-1, :]], axis=1)
            xr = mu_r * x + (1.0 - mu_r) * x_prev
            xk = mu_k * x + (1.0 - mu_k) * x_prev
            r = jax.nn.sigmoid(jnp.einsum('btc,dc->btd', xr, W_r))
            k = jnp.einsum('btc,dc->btd', xk, W_k)
            k_act = jnp.square(jax.nn.relu(k))
            out = r * jnp.einsum('btc,dc->btd', k_act, W_v)
            new_state = x[:, -1, :]
            return (out, new_state)
        key = jax.random.key(seed)
        ks = jax.random.split(key, 6)
        B, T, C = (8, 256, DIM)
        x = jax.random.normal(ks[0], (B, T, C), dtype=jnp.float32)
        s = 1.0 / np.sqrt(C)
        W_r = jax.random.uniform(ks[1], (C, C), jnp.float32, -s, s)
        W_k = jax.random.uniform(ks[2], (C, C), jnp.float32, -s, s)
        W_v = jax.random.uniform(ks[3], (C, C), jnp.float32, -s, s)
        mu_r = jax.random.uniform(ks[4], (C,), jnp.float32)
        mu_k = jax.random.uniform(ks[5], (C,), jnp.float32)
        return {'x': x, 'W_r': W_r, 'W_k': W_k, 'W_v': W_v, 'mu_r': mu_r, 'mu_k': mu_k}
    _L0_ffn_in = _L0_ffn_setup()
    _d = {'L0_attn_a_x': _L0_attn_a_in['x'], 'L0_attn_a_Wq': _L0_attn_a_in['Wq'], 'L0_attn_a_bq': _L0_attn_a_in['bq'], 'L0_attn_a_Wk': _L0_attn_a_in['Wk'], 'L0_attn_a_bk': _L0_attn_a_in['bk'], 'L0_attn_a_Wv': _L0_attn_a_in['Wv'], 'L0_attn_a_bv': _L0_attn_a_in['bv'], 'L0_attn_a_Wo': _L0_attn_a_in['Wo'], 'L0_attn_a_bo': _L0_attn_a_in['bo'], 'L0_attn_b_Wq': _L0_attn_b_in['Wq'], 'L0_attn_b_bq': _L0_attn_b_in['bq'], 'L0_attn_b_Wk': _L0_attn_b_in['Wk'], 'L0_attn_b_bk': _L0_attn_b_in['bk'], 'L0_attn_b_Wv': _L0_attn_b_in['Wv'], 'L0_attn_b_bv': _L0_attn_b_in['bv'], 'L0_attn_b_Wg': _L0_attn_b_in['Wg'], 'L0_attn_b_bg': _L0_attn_b_in['bg'], 'L0_attn_b_Wo': _L0_attn_b_in['Wo'], 'L0_attn_b_bo': _L0_attn_b_in['bo'], 'L0_attn_b_gamma': _L0_attn_b_in['gamma'], 'L0_attn_b_beta': _L0_attn_b_in['beta'], 'L0_ffn_W_r': _L0_ffn_in['W_r'], 'L0_ffn_W_k': _L0_ffn_in['W_k'], 'L0_ffn_W_v': _L0_ffn_in['W_v'], 'L0_ffn_mu_r': _L0_ffn_in['mu_r'], 'L0_ffn_mu_k': _L0_ffn_in['mu_k']}
    _x0 = _d['L0_attn_a_x']
    _d['L0_attn_a_x'] = jax.random.normal(jax.random.fold_in(jax.random.key(seed), 1), (8, 256, 128), dtype=_x0.dtype)
    del _x0
    return _d

def reference(L0_attn_a_x, L0_attn_a_Wq, L0_attn_a_bq, L0_attn_a_Wk, L0_attn_a_bk, L0_attn_a_Wv, L0_attn_a_bv, L0_attn_a_Wo, L0_attn_a_bo, L0_attn_b_Wq, L0_attn_b_bq, L0_attn_b_Wk, L0_attn_b_bk, L0_attn_b_Wv, L0_attn_b_bv, L0_attn_b_Wg, L0_attn_b_bg, L0_attn_b_Wo, L0_attn_b_bo, L0_attn_b_gamma, L0_attn_b_beta, L0_ffn_W_r, L0_ffn_W_k, L0_ffn_W_v, L0_ffn_mu_r, L0_ffn_mu_k):

    def _L0_attn_a_ref(x, Wq, bq, Wk, bk, Wv, bv, Wo, bo):
        import jax, jax.numpy as jnp
        import numpy as np
        EMB_DIM = 128
        N_HEADS = 16
        HEAD_DIM = EMB_DIM // N_HEADS
        SEQ = 256
        BSZ = 2

        def _rope_pair(q, k):
            bsz, seq_len, d_model = q.shape
            freq_range = jnp.arange(d_model // 2, dtype=jnp.float32)
            freq_cis = jnp.power(10000.0, -2.0 * freq_range / d_model)
            pos = jnp.arange(seq_len, dtype=jnp.float32)
            freq = jnp.einsum('i,j->ij', pos, freq_cis)
            sin_e = jnp.sin(freq)[None]
            cos_e = jnp.cos(freq)[None]
            q_even, q_odd = (q[..., ::2], q[..., 1::2])
            k_even, k_odd = (k[..., ::2], k[..., 1::2])
            q_rot = jnp.concatenate([q_even * cos_e - q_odd * sin_e, q_even * sin_e - q_odd * cos_e], axis=-1)
            k_rot = jnp.concatenate([k_even * cos_e - k_odd * sin_e, k_even * sin_e - k_odd * cos_e], axis=-1)
            return (q_rot, k_rot)
        bsz, n, d = x.shape
        Q = x @ Wq + bq
        K = x @ Wk + bk
        V = x @ Wv + bv
        Q, K = _rope_pair(Q, K)
        Q = Q.reshape(bsz, n, N_HEADS, HEAD_DIM).transpose(0, 2, 1, 3)
        K = K.reshape(bsz, n, N_HEADS, HEAD_DIM).transpose(0, 2, 1, 3)
        V = V.reshape(bsz, n, N_HEADS, HEAD_DIM).transpose(0, 2, 1, 3)
        scores = jnp.einsum('bhqd,bhkd->bhqk', Q, K)
        causal = jnp.triu(jnp.ones((n, n), dtype=bool), k=1)
        scores = jnp.where(causal, -jnp.inf, scores)
        attn = jax.nn.softmax(scores / jnp.sqrt(jnp.float32(HEAD_DIM)), axis=-1)
        ctx = jnp.einsum('bhqk,bhkd->bhqd', attn, V)
        ctx = ctx.transpose(0, 2, 1, 3).reshape(bsz, n, d)
        return ctx @ Wo + bo

    def _L0_attn_b_ref(x, Wq, bq, Wk, bk, Wv, bv, Wg, bg, Wo, bo, gamma, beta):
        import jax, jax.numpy as jnp
        import numpy as np
        import math
        D_MODEL = 128
        N_HEADS = 16
        D_HEAD = D_MODEL // N_HEADS
        DECAY_MAX = 0.99
        LN_EPS = 1e-05

        def _decay_mask(S):
            i = jnp.arange(S, dtype=jnp.float32)[:, None]
            j = jnp.arange(S, dtype=jnp.float32)[None, :]
            diff = i - j
            return jnp.where(diff >= 0, jnp.power(jnp.float32(DECAY_MAX), diff), 0.0)
        B, S, D = x.shape
        H, DH = (N_HEADS, D_HEAD)
        Q = (x @ Wq + bq).reshape(B, S, H, DH).transpose(0, 2, 1, 3)
        K = (x @ Wk + bk).reshape(B, S, H, DH).transpose(0, 2, 1, 3)
        V = (x @ Wv + bv).reshape(B, S, H, DH).transpose(0, 2, 1, 3)
        scores = jnp.einsum('bhsd,bhtd->bhst', Q, K) / math.sqrt(DH)
        mask = _decay_mask(S)
        retained = jnp.einsum('bhst,bhtd->bhsd', scores * mask, V)
        retained = retained.transpose(0, 2, 1, 3).reshape(B, S, D)
        mu = jnp.mean(retained, axis=-1, keepdims=True)
        var = jnp.var(retained, axis=-1, keepdims=True)
        normed = (retained - mu) * jax.lax.rsqrt(var + LN_EPS) * gamma + beta
        G = jax.nn.sigmoid(x @ Wg + bg)
        return normed * G @ Wo + bo

    def _L0_ffn_ref(x, W_r, W_k, W_v, mu_r, mu_k):
        import jax, jax.numpy as jnp
        import numpy as np
        DIM = 128

        def _reference_tuple_inner(x, W_r, W_k, W_v, mu_r, mu_k):
            B, T, C = x.shape
            x_prev = jnp.concatenate([jnp.zeros((B, 1, C), x.dtype), x[:, :-1, :]], axis=1)
            xr = mu_r * x + (1.0 - mu_r) * x_prev
            xk = mu_k * x + (1.0 - mu_k) * x_prev
            r = jax.nn.sigmoid(jnp.einsum('btc,dc->btd', xr, W_r))
            k = jnp.einsum('btc,dc->btd', xk, W_k)
            k_act = jnp.square(jax.nn.relu(k))
            out = r * jnp.einsum('btc,dc->btd', k_act, W_v)
            new_state = x[:, -1, :]
            return (out, new_state)
        return _reference_tuple_inner(x, W_r, W_k, W_v, mu_r, mu_k)[0]
    x = L0_attn_a_x
    x = x + _L0_attn_a_ref(_layernorm(x, axis=-1), L0_attn_a_Wq, L0_attn_a_bq, L0_attn_a_Wk, L0_attn_a_bk, L0_attn_a_Wv, L0_attn_a_bv, L0_attn_a_Wo, L0_attn_a_bo)
    x = x + _L0_ffn_ref(_layernorm(x, axis=-1), L0_ffn_W_r, L0_ffn_W_k, L0_ffn_W_v, L0_ffn_mu_r, L0_ffn_mu_k)
    x = x + _L0_attn_b_ref(_layernorm(x, axis=-1), L0_attn_b_Wq, L0_attn_b_bq, L0_attn_b_Wk, L0_attn_b_bk, L0_attn_b_Wv, L0_attn_b_bv, L0_attn_b_Wg, L0_attn_b_bg, L0_attn_b_Wo, L0_attn_b_bo, L0_attn_b_gamma, L0_attn_b_beta)
    x = x + _L0_ffn_ref(_layernorm(x, axis=-1), L0_ffn_W_r, L0_ffn_W_k, L0_ffn_W_v, L0_ffn_mu_r, L0_ffn_mu_k)
    return x

_drawn_inputs = setup_inputs


def setup_inputs(seed=0):
    import zlib

    import numpy as np

    out = dict(_drawn_inputs(seed))
    spreads = {'L0_attn_b_bq': (0.0, 0.1),
     'L0_attn_b_bk': (0.0, 0.1),
     'L0_attn_b_bv': (0.0, 0.1),
     'L0_attn_b_bg': (0.0, 0.8),
     'L0_attn_b_bo': (0.0, 0.1),
     'L0_attn_b_gamma': (1.0, 0.6),
     'L0_attn_b_beta': (0.0, 0.68)}
    factors = {'L0_attn_a_bq': 8.0, 'L0_attn_a_bk': 26.437, 'L0_attn_b_Wg': 4.564, 'L0_ffn_mu_r': 3.262}
    for name, (base, spread) in spreads.items():
        noise = np.random.default_rng([zlib.crc32(name.encode()), seed]).standard_normal(out[name].shape)
        drawn = base * np.exp(spread * noise) if base else spread * noise
        out[name] = jnp.asarray(drawn.astype(out[name].dtype))
    for name, factor in factors.items():
        out[name] = (out[name] * factor).astype(out[name].dtype)
    return out
```

```python
from contextlib import ExitStack

import concourse.bass as bass
from concourse import mybir
import numpy as np

ALU = mybir.AluOpType
ACT = mybir.ActivationFunctionType
AX_X = mybir.AxisListType.X
F32 = mybir.dt.float32
BF16 = mybir.dt.bfloat16

B, S, D = 8, 256, 128
P = 128
T = S // P
H, HD = 16, 8
PARTS = 3
PAIRS = PARTS * PARTS
ROWS = HD * PAIRS
XROWS = ROWS + PARTS
SLOT = HD + 1
CT = 32
NCT = P // CT
SCALE = float(HD) ** -0.5
DECAY = 0.99
EPS = 1e-5
BIG = 1e30
QKW = 2 * D
STAGES = 4


def constants():
    freq = np.power(np.float32(10000.0), np.float32(-2.0) * np.arange(D // 2, dtype=np.float32) / np.float32(D))
    ang = (np.arange(S, dtype=np.float32)[:, None] * freq.astype(np.float32)[None, :]).astype(np.float32)
    cos, sin = np.cos(ang), np.sin(ang)

    def rope(first, second):
        t = np.concatenate([first, second], axis=1).reshape(T, P, 1, D)
        return np.repeat(t, 2, axis=2).transpose(1, 0, 2, 3).reshape(P, T * 2 * D).astype(np.float32)

    i = np.arange(P)
    diff = (i[None, :] - i[:, None]).astype(np.float32)
    power = np.power(np.float32(DECAY), np.abs(diff)).astype(np.float32)
    decay = np.where(diff >= 0, power, 0.0).astype(np.float32) * np.float32(SCALE)
    same_head = (i[:, None] % H == i[None, :] // HD).astype(np.float32)
    key_decay = np.power(np.float64(DECAY), P - 1 - i).astype(np.float32)[:, None]
    query_decay = np.tile((np.power(np.float64(DECAY), i + 1) * SCALE).astype(np.float32)[None, :], (P, 1))
    future = np.where(i[None, :] > i[:, None], -BIG, 0.0)
    return {
        "c_rope": np.concatenate([rope(cos, sin), rope(sin, cos)], axis=1),
        "c_f32": np.concatenate([np.eye(P, dtype=np.float32), decay, same_head, query_decay, key_decay], axis=1),
        "c_bf16": np.concatenate([np.eye(P), np.tile(future, (1, 4))], axis=1).astype(np.float32),
    }


def build(nc, x, a, b, f, c, out):
    ctx = ExitStack()
    with ctx:
        def sb(name, shape, dt=F32):
            return ctx.enter_context(nc.sbuf_tensor(name, shape, dt))

        def sem(name):
            return ctx.enter_context(nc.semaphore(name))

        rope = sb("rope", [P, 2, T * QKW])
        cf = sb("cf", [P, 4 * P + 1])
        cb = sb("cb", [P, P + 4 * P], BF16)
        ident, decay, same_head, query_decay = (cf[:, n * P:(n + 1) * P] for n in range(4))
        key_decay = cf[:, 4 * P:4 * P + 1]
        identb, future = cb[:, 0:P], cb[:, P:5 * P]
        wa = sb("wa", [P, 4, D])
        wb = sb("wb", [P, 5, D])
        wqk_dh = sb("wqk_dh", [P, 2, D])
        wf = sb("wf", [P, 3, D])
        wfT = sb("wfT", [P, 3, D])
        vecs = sb("vecs", [P, 7])
        half = sb("half", [P, 3])
        NB = 6
        brow = sb("brow", [1, 3, NB * D])
        browp = sb("browp", [1, PARTS, NB * D], BF16)
        bias = sb("bias", [PARTS, NB * D], BF16)
        minus_half = sb("minus_half", [P, T])
        ones3 = sb("ones3", [PARTS, P], BF16)

        x_in = sb("x_in", [P, T, D])
        zA = sb("zA", [P, T, D])
        zAT = sb("zAT", [P, S])
        prod = sb("prod", [P, 2, T * QKW])
        rot = sb("rot", [P, T, 2, D])
        partsA = sb("partsA", [P, PARTS, 2 * S], BF16)
        remA = sb("remA", [P, 2 * S])
        Qst = sb("Qst", [XROWS, H, S], BF16)
        Kst = sb("Kst", [XROWS, H, S], BF16)
        mx = sb("mx", [P, T, H])
        mrem = sb("mrem", [P, T, H])
        maxp = sb("maxp", [P, T, PARTS, H], BF16)
        maxT = sb("maxT", [PARTS * H, S], BF16)
        VA = sb("VA", [P, T, H, CT])
        x_res = sb("x_res", [P, T, D])
        P0 = sb("P0", [P, H, S])
        P1 = sb("P1", [P, H, P])
        oA = sb("oA", [P, 2 * S])
        rsum = sb("rsum", [P, T * H // 2, 2])
        ctxA = sb("ctxA", [P, T, D])
        ctxT = sb("ctxT", [P, S])
        x1 = sb("x1", [P, T, D])
        x2 = sb("x2", [P, T, D])
        zB = sb("zB", [P, T, D])
        zBT = sb("zBT", [P, S])
        qkB = sb("qkB", [P, 2, S])
        partsB = sb("partsB", [P, PARTS, 2 * S], BF16)
        remB = sb("remB", [P, 2 * S])
        Rq = sb("Rq", [ROWS, H, S], BF16)
        Rk = sb("Rk", [ROWS, H, S], BF16)
        VB = sb("VB", [P, T, H, CT])
        gate = sb("gate", [P, S])
        kdec = sb("kdec", [P, D])
        qdec = sb("qdec", [P, P])
        state = sb("state", [P, D])
        x2_res = sb("x2_res", [P, T, D])
        PR = sb("PR", [P, T, H, P])
        oB = sb("oB", [P, S])
        zR = sb("zR", [P, T, D])
        nT = sb("nT", [P, S])
        yT = sb("yT", [P, S])
        x3 = sb("x3", [P, T, D])
        x4 = sb("x4", [P, T, D])

        bank = [ctx.enter_context(nc.psum_tensor(f"bank{n}", [P, 512], F32)) for n in range(8)]
        ring = bank[0:2]
        exp_ring = bank[2:4]
        b_o, b_1, b_3, b_4 = bank[4:8]

        class Norm:
            def __init__(self, name):
                self.st = sb(f"{name}_st", [P, T, 6])
                self.mv = sb(f"{name}_mv", [P, T, 2])
                self.var = sb(f"{name}_var", [P, T])
                self.rstd = sb(f"{name}_rstd", [P, T])
                self.stats, self.moments, self.shifted, self.rdev, self.done = (
                    sem(f"{name}_{n}") for n in ("stats", "moments", "shifted", "rdev", "done"))

        norm_a, norm_f1, norm_b, norm_r, norm_f2 = (Norm(n) for n in ("norm_a", "norm_f1", "norm_b", "norm_r", "norm_f2"))

        class Ffn:
            def __init__(self, name, norm, src, dst, psum):
                self.norm, self.src, self.dst, self.psum = norm, src, dst, psum
                self.z = sb(f"{name}_z", [P, T, D])
                self.zT = sb(f"{name}_zT", [P, 1 + S])
                self.dz = sb(f"{name}_dz", [P, S])
                self.mix = sb(f"{name}_mix", [P, 2, S])
                self.kr = sb(f"{name}_kr", [P, S])
                self.ka = sb(f"{name}_ka", [P, S])
                self.th = sb(f"{name}_th", [P, T, D])
                self.u = sb(f"{name}_u", [P, T, D])
                self.turned = sem(f"{name}_turned")
                self.zT_ready = sem(f"{name}_zT_ready")
                self.dz_ready = sem(f"{name}_dz_ready")
                self.mixed = sem(f"{name}_mixed")
                self.rk_ready = sem(f"{name}_rk_ready")
                self.relu_done = sem(f"{name}_relu_done")
                self.tanh_done = sem(f"{name}_tanh_done")
                self.squared = sem(f"{name}_squared")
                self.v_ready = sem(f"{name}_v_ready")
                self.gated = sem(f"{name}_gated")
                self.x_ready = sem(f"{name}_x_ready")

        f1 = Ffn("f1", norm_f1, x1, x2, b_3)
        f2 = Ffn("f2", norm_f2, x3, x4, b_4)

        tables_in, biases_in, bias_rows_in, wf_in = sem("tables_in"), sem("biases_in"), sem("bias_rows_in"), sem("wf_in")
        masks_ready = sem("masks_ready")
        bias_split, cleared, wf_turned, wf_ready, halved = (sem(n) for n in ("bias_split", "cleared", "wf_turned", "wf_ready", "halved"))
        xin_in, zAT_psum, zAT_ready, qkA_psum, products, rotated = (
            sem(n) for n in ("xin_in", "zAT_psum", "zAT_ready", "qkA_psum", "products", "rotated"))
        rotT_psum, splitA, splitA_rem, stackA_in, vA_psum, vA_ready = (
            sem(n) for n in ("rotT_psum", "splitA", "splitA_rem", "stackA_in", "vA_psum", "vA_ready"))
        scores_full, scores_max, maxp_step, maxp_ready, maxT_psum, maxT_ready, max_rows_in = (
            sem(n) for n in ("scores_full", "scores_max", "maxp_step", "maxp_ready", "maxT_psum", "maxT_ready", "max_rows_in"))
        st_full, exp_done, masked, pv_done, oA_ready, oAT_psum, rsum_ready, ctx_ready, ctxT_psum, ctxT_ready, projA, x1_ready = (
            sem(n) for n in ("st_full", "exp_done", "masked", "pv_done", "oA_ready", "oAT_psum", "rsum_ready", "ctx_ready",
                             "ctxT_psum", "ctxT_ready", "projA", "x1_ready"))
        xres_in, zBT_psum, zBT_ready, qkB_psum, qkB_ready, splitB, splitB_rem, stackB_in = (
            sem(n) for n in ("xres_in", "zBT_psum", "zBT_ready", "qkB_psum", "qkB_ready", "splitB", "splitB_rem", "stackB_in"))
        vg_psum, vB_ready, gate_ready, kB_psum, kdec_ready, qdec_ready, kv_psum, state_ready, x2_copied = (
            sem(n) for n in ("vg_psum", "vB_ready", "gate_ready", "kB_psum", "kdec_ready", "qdec_ready", "kv_psum", "state_ready", "x2_copied"))
        ret_full, ret_done, oB_psum, oB_ready, oBT_psum, zRT_psum, nT_ready, yT_ready, projB, out_done = (
            sem(n) for n in ("ret_full", "ret_done", "oB_psum", "oB_ready", "oBT_psum", "zRT_psum", "nT_ready", "yT_ready", "projB", "out_done"))

        NFILL = T * H * P * T // 512 - H * P // 512
        NRET = T * H * P // 512
        NSTACK = 1 + PARTS

        def running(s, stage):
            return not isinstance(s, int) or 0 <= s - stage < B

        passed = {e: sem(f"passed_{e}") for e in ("pe", "dve", "pool", "sp")}

        def apart(eng, name):
            eng.sem_inc(passed[name], 1)

        def slots(eng, body):
            for s in range(STAGES):
                body(s)
            with eng.Fori(STAGES, B) as s:
                body(s)
            for s in range(B, B + STAGES - 1):
                body(s)

        def hs(set_, j, n):
            return set_ * 8 + 2 * j + n

        EXP_FILLS = [(half_, kt, h) for half_ in range(2) for kt, n in ((0, 2), (1, 4)) for h in range(8 * half_, 8 * half_ + 8, n)]

        scratchA, scratchB = ([nc.dram_tensor(f"parts_{w}_{n}", (PARTS, D, S), BF16, kind="Internal").ap() for n in "qk"] for w in "ab")
        spilledA, spilledB, projB_used = sem("spilledA"), sem("spilledB"), sem("projB_used")

        block = ctx.enter_context(nc.Block())

        def pair_view(v):
            whole = v[:, :, :, :]
            return bass.AP(whole.tensor, whole.offset, [whole.ap[0], [2 * CT, T * H // 2], [CT + SLOT, 2], [1, HD]])

        def quad_view(v):
            whole = v[:, :, :, :]
            return bass.AP(whole.tensor, whole.offset, [whole.ap[0], [4 * CT, T * H // 4], [CT + HD, 4], [1, HD]])

        @block.sync
        def _(sp):
            sp.dma_start(rope[:, :, :], c["c_rope"].rearrange("p (a n) -> p a n", a=2)).then_inc(tables_in, 16)
            sp.dma_start(cf[:, :], c["c_f32"]).then_inc(tables_in, 16)
            sp.dma_start(prod[:, :, :].rearrange("p a n -> p (a n)")[:, 0:5 * P], c["c_bf16"]).then_inc(tables_in, 16)
            for n, w in enumerate((a["Wq"], a["Wk"], a["Wv"], a["Wo"])):
                sp.dma_start(wa[:, n, :], w).then_inc(tables_in, 16)
            for n, w in enumerate((b["Wq"], b["Wk"], b["Wv"], b["Wg"], b["Wo"])):
                sp.dma_start(wb[:, n, :], w).then_inc(tables_in, 16)
            for n, w in enumerate((f["W_r"], f["W_k"], f["W_v"])):
                sp.dma_start(wf[:, n, :], w).then_inc(tables_in, 16)
            for n, w in enumerate((a["bq"], a["bk"], a["bv"], a["bo"], b["bv"], b["bo"])):
                sp.dma_start(brow[0:1, 0, n * D:(n + 1) * D], w.rearrange("(o n) -> o n", o=1)).then_inc(biases_in, 16)
            with nc.allow_non_contiguous_dma(reason="seven vectors onto partitions, once"):
                for n, w in enumerate((f["mu_r"], f["mu_k"], b["bg"], b["gamma"], b["beta"])):
                    sp.dma_start(vecs[:, n:n + 1], w.rearrange("(n o) -> n o", o=1)).then_inc(biases_in, 16)
                for n, w in enumerate((b["bq"], b["bk"])):
                    for d in range(HD):
                        sp.dma_start(vecs[d * H:(d + 1) * H, 5 + n:6 + n], w.rearrange("(h d) -> h d", d=HD)[:, d:d + 1]).then_inc(biases_in, 16)
            sp.wait_ge(bias_split, 5)
            for n in range(PARTS):
                sp.dma_start(bias[n:n + 1, :], browp[0:1, n, :]).then_inc(bias_rows_in, 16)

            def load_x(i):
                if not (isinstance(i, int) and i == 0):
                    sp.wait_ge(norm_a.done, i)
                sp.dma_start(x_in[:, :, :], x[i].rearrange("(t p) d -> p t d", p=P)).then_inc(xin_in, 16)

            def load_x_res(i):
                sp.wait_ge(x1_ready, i)
                sp.dma_start(x_res[:, :, :], x[i].rearrange("(t p) d -> p t d", p=P)).then_inc(xres_in, 16)

            def spill(parts, scratch, spilled):
                for n in range(2):
                    sp.dma_start(scratch[n].rearrange("m r t -> r m t"), parts[:, :, n * S:(n + 1) * S]).then_inc(spilled, 16)

            def stacks(q_st, k_st, i, scratch, spilled, landed):
                sp.wait_ge(spilled, 32 * (i + 1))
                q_d, k_d = scratch
                sp.dma_start(k_st[0:ROWS, :, :], k_d.rearrange("m (d h) t -> (m d) (h t)", d=HD).unsqueeze(0)
                             .to_broadcast([PARTS, PARTS * HD, H * S])).then_inc(landed, 16)
                for n in range(PARTS):
                    rows = slice(n * PARTS * HD, (n + 1) * PARTS * HD)
                    sp.dma_start(q_st[rows, :, :], q_d[n].rearrange("(d h) t -> d (h t)", d=HD).unsqueeze(0)
                                 .to_broadcast([PARTS, HD, H * S])).then_inc(landed, 16)

            def slot(s):
                if running(s, 0):
                    load_x(s)
                if running(s, 1):
                    load_x_res(s - 1)
                if running(s, 3):
                    i = s - 3
                    sp.wait_ge(projB_used, i)
                    apart(sp, "sp")
                    sp.wait_ge(f1.x_ready, i + 1)
                    sp.dma_start(x2_res[:, :, :], x2[:, :, :]).then_inc(x2_copied, 16)
                if running(s, 0):
                    sp.wait_ge(splitA, 3 * (s + 1))
                    spill(partsA, scratchA, spilledA)
                    if running(s, 1):
                        sp.wait_ge(st_full, NFILL * s)
                        apart(sp, "sp")
                    stacks(Qst, Kst, s, scratchA, spilledA, stackA_in)
                if running(s, 2):
                    i = s - 2
                    sp.wait_ge(splitB, 3 * (i + 1))
                    spill(partsB, scratchB, spilledB)
                    sp.wait_ge(ret_full, NRET * i)
                    apart(sp, "sp")
                    stacks(Rq, Rk, i, scratchB, spilledB, stackB_in)
                if running(s, 0):
                    sp.wait_ge(maxT_ready, s + 1)
                    for n in range(PARTS):
                        sp.dma_start(Qst[ROWS + n:ROWS + n + 1, :, :], maxT[n * H:(n + 1) * H, :]).then_inc(max_rows_in, 16)
                if running(s, 3):
                    i = s - 3
                    sp.wait_ge(f2.x_ready, i + 1)
                    sp.dma_start(out[i].rearrange("(t p) d -> p t d", p=P), x4[:, :, :]).then_inc(out_done, 16)

            slots(sp, slot)
            sp.wait_ge(out_done, 16 * B)

        @block.gpsimd
        def _(pool):
            pool.memset(VA[:, :, :, :], 0.0).then_inc(cleared, 1)
            pool.memset(VB[:, :, :, :], 0.0).then_inc(cleared, 1)
            pool.memset(ones3[:, :], 1.0).then_inc(cleared, 1)
            pool.wait_ge(cleared, 3)
            pool.memset(Kst[64:XROWS, :, :], -1.0).then_inc(cleared, 1)
            pool.wait_ge(cleared, 4)
            pool.memset(f1.zT[:, 0:1], 0.0).then_inc(cleared, 1)
            pool.memset(f2.zT[:, 0:1], 0.0).then_inc(cleared, 1)
            pool.memset(minus_half[:, :], -0.5).then_inc(cleared, 1)
            pool.wait_ge(cleared, 7)
            va = VA[:, :, :, :].rearrange("p t (g n) c -> p (t g) n c", n=2)
            for n in range(2):
                pool.memset(va[:, :, n, n * SLOT + HD:n * SLOT + HD + 1], 1.0).then_inc(cleared, 1)
            pool.wait_ge(tables_in, 16 * 15)
            for n in range(2):
                pool.tensor_copy(wqk_dh[:, n, :].rearrange("c (d h) -> c h d", h=H), wb[:, n, :].rearrange("c (h d) -> c h d", d=HD)).then_inc(cleared, 1)

            def deviation(N, i):
                pool.wait_ge(N.moments, i + 1)
                apart(pool, "pool")
                pool.tensor_scalar(N.var[:, :], N.mv[:, :, 1], EPS, None, ALU.add).then_inc(N.shifted, 1)
                pool.wait_ge(N.shifted, i + 1)
                pool.wait_ge(N.done, i)
                pool.tensor_tensor(N.rstd[:, :], N.var[:, :], minus_half[:, :], ALU.pow).then_inc(N.rdev, 1)

            def rotate(i):
                pool.wait_ge(products, 2 * (i + 1))
                pool.wait_ge(rotT_psum, i)
                turned = rot[:, :, :, :].rearrange("p t w (d h) -> p (t w) h d", h=H)
                first, second = (prod[:, n, :].rearrange("p (w h d) -> p w h d", w=2 * T, d=HD) for n in range(2))
                pool.tensor_tensor(turned, first, second, ALU.subtract).then_inc(rotated, 1)

            def split_max(i):
                pool.wait_ge(scores_max, NFILL * (i + 1))
                pool.wait_ge(maxT_psum, i)
                apart(pool, "pool")
                pool.tensor_copy(maxp[:, :, 0, :], mx[:, :, :]).then_inc(maxp_step, 1)
                pool.wait_ge(maxp_step, 3 * i + 1)
                pool.tensor_tensor(mrem[:, :, :], mx[:, :, :], maxp[:, :, 0, :], ALU.subtract).then_inc(maxp_step, 1)
                pool.wait_ge(maxp_step, 3 * i + 2)
                apart(pool, "pool")
                pool.tensor_copy(maxp[:, :, 1, :], mrem[:, :, :]).then_inc(maxp_step, 1)
                pool.wait_ge(maxp_step, 3 * i + 3)
                pool.tensor_tensor(maxp[:, :, 2, :], mrem[:, :, :], maxp[:, :, 1, :], ALU.subtract).then_inc(maxp_ready, 1)

            def mask(i, g):
                _, kt, h = EXP_FILLS[g]
                pool.wait_ge(exp_done, NFILL * i + g + 1)
                apart(pool, "pool")
                blockp = P0[:, h:h + 2, 0:P] if kt == 0 else P1[:, h:h + 4, :]
                pool.affine_select(out=blockp, in_=blockp, compare_op=ALU.is_ge, fill=0.0, base=0,
                                   pattern=[[0, blockp.shape[1]], [1, P]], channel_multiplier=-1).then_inc(masked, 1)

            def square(F, i):
                pool.wait_ge(F.relu_done, i + 1)
                pool.tensor_tensor(F.ka[:, :], F.kr[:, :], F.kr[:, :], ALU.mult).then_inc(F.squared, 1)

            def decay_q(i):
                pool.wait_ge(qkB_ready, 2 * (i + 1))
                pool.wait_ge(oB_psum, i)
                pool.tensor_tensor(qdec[:, :], qkB[:, 0, P:S], query_decay, ALU.mult).then_inc(qdec_ready, 1)

            def slot(s):
                one, two, three, four = (running(s, n) for n in range(4))
                if one:
                    deviation(norm_a, s)
                if three:
                    deviation(norm_f1, s - 2)
                for g in range(NFILL):
                    if two:
                        mask(s - 1, g)
                    if g == 1 and one:
                        rotate(s)
                    if g == 5 and three:
                        square(f1, s - 2)
                if three:
                    deviation(norm_b, s - 2)
                if four:
                    deviation(norm_r, s - 3)
                if three:
                    decay_q(s - 2)
                if four:
                    deviation(norm_f2, s - 3)
                    square(f2, s - 3)
                if one:
                    split_max(s)

            slots(pool, slot)

        @block.scalar
        def _(act):
            act.wait_ge(biases_in, 16 * (NB + 5 + 2 * HD))
            act.mul(half[:, :], vecs[:, 2:5], 0.5).then_inc(halved, 1)
            act.wait_ge(wf_turned, 1)
            act.activation(wfT[:, :, :].rearrange("p a n -> p (a n)"), b_3[:, 0:3 * D], ACT.Copy).then_inc(wf_ready, 1)
            act.wait_ge(halved, 1)
            act.wait_ge(cleared, 9)

            def norm_turn(i):
                act.wait_ge(zAT_psum, i + 1)
                act.activation(zAT[:, :], b_1[:, 0:S], ACT.Copy).then_inc(zAT_ready, 1)

            def split_a(i):
                act.wait_ge(rotT_psum, i + 1)
                act.wait_ge(stackA_in, 16 * NSTACK * i)
                act.activation(partsA[:, 0, :], b_1[:, :], ACT.Copy).then_inc(splitA, 1)
                act.wait_ge(splitA_rem, i + 1)
                act.activation(partsA[:, 1, :], remA[:, :], ACT.Copy).then_inc(splitA, 1)

            def v_a(i):
                act.wait_ge(vA_psum, i + 1)
                act.wait_ge(pv_done, 2 * i)
                act.activation(pair_view(VA), b_1[:, 0:T * D].rearrange("p (g n d) -> p g n d", n=2, d=HD), ACT.Copy).then_inc(vA_ready, 1)

            def max_turn(i):
                act.wait_ge(maxT_psum, i + 1)
                act.wait_ge(max_rows_in, 16 * PARTS * i)
                act.activation(maxT[:, :], b_1[0:PARTS * H, 0:S // 2].bitcast(BF16), ACT.Copy).then_inc(maxT_ready, 1)

            def exps(i, g):
                _, kt, h = EXP_FILLS[g]
                act.wait_ge(st_full, NFILL * i + g + 1)
                if g == 0:
                    act.wait_ge(pv_done, 2 * i)
                dst = P0[:, h:h + 2, :] if kt == 0 else P1[:, h:h + 4, :]
                act.activation(dst.rearrange("p h q -> p (h q)"), exp_ring[g % 2][:, :], ACT.Exp, scale=SCALE).then_inc(exp_done, 1)

            def o_a(i):
                act.wait_ge(pv_done, 2 * (i + 1))
                act.activation(oA[:, :], b_o[:, :], ACT.Copy).then_inc(oA_ready, 1)

            def ctx_turn(i):
                act.wait_ge(ctxT_psum, i + 1)
                act.activation(ctxT[:, :], b_o[:, 0:S], ACT.Copy).then_inc(ctxT_ready, 1)

            def ffn_zT(F, i):
                act.wait_ge(F.turned, i + 1)
                act.activation(F.zT[:, 1:1 + S], F.psum[:, 0:S], ACT.Copy).then_inc(F.zT_ready, 1)

            def ffn_act(F, i):
                act.wait_ge(F.rk_ready, i + 1)
                act.activation(F.kr[:, :], F.psum[:, 0:S], ACT.Relu).then_inc(F.relu_done, 1)
                act.activation(F.th[:, :, :].rearrange("p t d -> p (t d)"), F.psum[:, S:2 * S], ACT.Tanh, scale=0.5).then_inc(F.tanh_done, 1)

            def b_turn(i):
                act.wait_ge(zBT_psum, i + 1)
                act.activation(zBT[:, :], b_3[:, 0:S], ACT.Copy).then_inc(zBT_ready, 1)

            def b_qk(i):
                act.wait_ge(qkB_psum, i + 1)
                for n in range(2):
                    act.activation(qkB[:, n, :], b_3[:, n * S:(n + 1) * S], ACT.Identity, bias=vecs[:, 5 + n:6 + n]).then_inc(qkB_ready, 1)
                act.wait_ge(qkB_ready, 2 * (i + 1))
                act.wait_ge(stackB_in, 16 * NSTACK * i)
                act.activation(partsB[:, 0, :], qkB[:, :, :].rearrange("p n s -> p (n s)"), ACT.Copy).then_inc(splitB, 1)
                act.wait_ge(splitB_rem, i + 1)
                act.activation(partsB[:, 1, :], remB[:, :], ACT.Copy).then_inc(splitB, 1)

            def b_vg(i):
                act.wait_ge(vg_psum, i + 1)
                act.wait_ge(oB_psum, i)
                act.activation(quad_view(VB), b_3[:, 0:T * D].rearrange("p (g n d) -> p g n d", n=4, d=HD), ACT.Copy).then_inc(vB_ready, 1)
                act.wait_ge(yT_ready, i)
                act.activation(gate[:, :], b_3[:, S:2 * S], ACT.Tanh, bias=half[:, 0:1], scale=0.5).then_inc(gate_ready, 1)

            def b_k(i):
                act.wait_ge(kB_psum, i + 1)
                act.activation(kdec[:, :], b_3[:, 0:D], ACT.Copy, scale=key_decay).then_inc(kdec_ready, 1)

            def o_b(i):
                act.wait_ge(oB_psum, i + 1)
                act.activation(oB[:, :], b_4[:, 0:S], ACT.Copy).then_inc(oB_ready, 1)

            def affine_b(i):
                act.wait_ge(zRT_psum, i + 1)
                act.activation(nT[:, :], b_4[:, 0:S], ACT.Identity, bias=half[:, 2:3], scale=half[:, 1:2]).then_inc(nT_ready, 1)

            def slot(s):
                one, two, three, four = (running(s, n) for n in range(4))
                if one:
                    norm_turn(s)
                if three:
                    ffn_zT(f1, s - 2)
                for g in range(NFILL):
                    if two:
                        exps(s - 1, g)
                    if g == 4 and three:
                        ffn_act(f1, s - 2)
                    if g == 7 and one:
                        split_a(s)
                if three:
                    b_turn(s - 2)
                if four:
                    o_b(s - 3)
                if two:
                    o_a(s - 1)
                if one:
                    v_a(s)
                if three:
                    b_qk(s - 2)
                if two:
                    ctx_turn(s - 1)
                if four:
                    affine_b(s - 3)
                if three:
                    b_vg(s - 2)
                if four:
                    ffn_zT(f2, s - 3)
                if three:
                    b_k(s - 2)
                if four:
                    ffn_act(f2, s - 3)
                if one:
                    max_turn(s)

            slots(act, slot)

        @block.vector
        def _(dve):
            def norm(N, src, z, i, first=None):
                if first is not None:
                    first()
                for t in range(T):
                    ins = dve.bn_stats(N.st[:, t, :], src[:, t, :])
                ins.then_inc(N.stats, 1)
                dve.wait_ge(N.stats, i + 1)
                apart(dve, "dve")
                for t in range(T):
                    ins = dve.bn_aggr(N.mv[:, t, :], N.st[:, t, :])
                ins.then_inc(N.moments, 1)
                dve.wait_ge(N.rdev, i + 1)
                for t in range(T):
                    ins = dve.tensor_scalar(z[:, t, :], src[:, t, :], N.mv[:, t, 0:1], N.rstd[:, t:t + 1], ALU.subtract, ALU.mult)
                ins.then_inc(N.done, 1)

            dve.wait_ge(biases_in, 16 * (NB + 5 + 2 * HD))
            dve.tensor_copy(browp[0:1, 0, :], brow[0:1, 0, :]).then_inc(bias_split, 1)
            for n in range(PARTS - 1):
                dve.wait_ge(bias_split, 2 * n + 1)
                dve.tensor_tensor(brow[0:1, n + 1, :], brow[0:1, n, :], browp[0:1, n, :], ALU.subtract).then_inc(bias_split, 1)
                dve.wait_ge(bias_split, 2 * n + 2)
                dve.tensor_copy(browp[0:1, n + 1, :], brow[0:1, n + 1, :]).then_inc(bias_split, 1)
            dve.wait_ge(tables_in, 16 * 15)
            dve.tensor_copy(cb[:, :], prod[:, :, :].rearrange("p a n -> p (a n)")[:, 0:5 * P]).then_inc(masks_ready, 1)

            def norm_of_a(i):
                dve.wait_ge(xin_in, 16 * (i + 1))
                dve.wait_ge(zAT_psum, i)
                norm(norm_a, x_in, zA, i)

            def rope_products(i):
                dve.wait_ge(qkA_psum, i + 1)
                dve.wait_ge(rotated, i)
                qk = b_1[:, :].rearrange("p (w f e) -> p w f e", w=2 * T, e=2)
                for n in range(2):
                    src = qk[:, :, :, n].unsqueeze(2).to_broadcast([P, 2 * T, 2, D // 2])
                    dve.tensor_tensor(prod[:, n, :].rearrange("p (w c f) -> p w c f", w=2 * T, c=2), src,
                                      rope[:, n, :].rearrange("p (w c f) -> p w c f", w=2 * T, c=2), ALU.mult).then_inc(products, 1)

            def rest_a(i):
                dve.wait_ge(splitA, 3 * i + 1)
                dve.tensor_tensor(remA[:, :], b_1[:, :], partsA[:, 0, :], ALU.subtract).then_inc(splitA_rem, 1)

            def last_a(i):
                dve.wait_ge(splitA, 3 * i + 2)
                dve.wait_ge(splitA_rem, i + 1)
                dve.tensor_tensor(partsA[:, 2, :], remA[:, :], partsA[:, 1, :], ALU.subtract).then_inc(splitA, 1)

            def row_max(i, k):
                dve.wait_ge(scores_full, NFILL * i + k + 1)
                if k == 0:
                    dve.wait_ge(maxp_ready, i)
                if k < 4:
                    dve.tensor_reduce(mx[:, 0, 4 * k:4 * k + 4], ring[k % 2][:, :].rearrange("p (h k) -> p h k", h=4), AX_X, ALU.max).then_inc(scores_max, 1)
                else:
                    h = 2 * (k - 4)
                    dve.tensor_reduce(mx[:, 1, h:h + 2], ring[k % 2][:, :].rearrange("p (h k) -> p h k", h=2), AX_X, ALU.max).then_inc(scores_max, 1)

            def normalise(i):
                dve.wait_ge(oAT_psum, i + 1)
                whole = b_o[:, :]
                sums = bass.AP(whole.tensor, whole.offset + HD, [whole.ap[0], [CT, T * H // 2], [SLOT, 2]])
                vals = bass.AP(whole.tensor, whole.offset, [whole.ap[0], [CT, T * H // 2], [SLOT, 2], [1, HD]])
                dve.reciprocal(rsum[:, :, :], sums).then_inc(rsum_ready, 1)
                dve.wait_ge(rsum_ready, i + 1)
                dve.tensor_tensor(ctxA[:, :, :].rearrange("p t (g n d) -> p (t g) n d", n=2, d=HD), vals,
                                  rsum[:, :, :].unsqueeze(3).to_broadcast([P, T * H // 2, 2, HD]), ALU.mult).then_inc(ctx_ready, 1)

            def residual_a(i):
                dve.wait_ge(projA, i + 1)
                dve.wait_ge(xres_in, 16 * (i + 1))
                dve.wait_ge(f1.x_ready, i)
                dve.tensor_tensor(x1[:, :, :].rearrange("p t d -> p (t d)"), x_res[:, :, :].rearrange("p t d -> p (t d)"),
                                  b_o[:, S:2 * S], ALU.add).then_inc(x1_ready, 1)

            def ffn_mix(F, i):
                dve.wait_ge(F.zT_ready, i + 1)
                now, before = F.zT[:, 1:1 + S], F.zT[:, 0:S]
                dve.tensor_tensor(F.dz[:, :], now, before, ALU.subtract).then_inc(F.dz_ready, 1)
                dve.wait_ge(F.dz_ready, i + 1)
                for n in range(2):
                    dve.scalar_tensor_tensor(out=F.mix[:, n, :], in0=F.dz[:, :], scalar=vecs[:, n:n + 1], in1=before,
                                             op0=ALU.mult, op1=ALU.add).then_inc(F.mixed, 1)

            def ffn_out(F, i, free):
                dve.wait_ge(F.v_ready, i + 1)
                dve.wait_ge(F.tanh_done, i + 1)
                flat = lambda v: v[:, :, :].rearrange("p t d -> p (t d)")
                dve.scalar_tensor_tensor(out=flat(F.u), in0=flat(F.th), scalar=1.0, in1=F.psum[:, 0:S],
                                         op0=ALU.add, op1=ALU.mult).then_inc(F.gated, 1)
                dve.wait_ge(F.gated, i + 1)
                free(i)
                dve.scalar_tensor_tensor(out=flat(F.dst), in0=flat(F.u), scalar=0.5, in1=flat(F.src),
                                         op0=ALU.mult, op1=ALU.add).then_inc(F.x_ready, 1)

            def norm_of_f1(i):
                dve.wait_ge(x1_ready, i + 1)
                norm(norm_f1, x1, f1.z, i)

            def norm_of_b(i):
                dve.wait_ge(f1.x_ready, i + 1)
                norm(norm_b, x2, zB, i)

            def rest_b(i):
                dve.wait_ge(splitB, 3 * i + 1)
                dve.tensor_tensor(remB[:, :], qkB[:, :, :].rearrange("p n s -> p (n s)"), partsB[:, 0, :], ALU.subtract).then_inc(splitB_rem, 1)
                dve.wait_ge(splitB_rem, i + 1)
                dve.wait_ge(splitB, 3 * i + 2)
                dve.tensor_tensor(partsB[:, 2, :], remB[:, :], partsB[:, 1, :], ALU.subtract).then_inc(splitB, 1)

            def keep_heads(i):
                dve.wait_ge(kv_psum, i + 1)
                dve.wait_ge(oB_psum, i)
                dve.tensor_tensor(state[:, :], b_3[:, D:2 * D], same_head, ALU.mult).then_inc(state_ready, 1)

            def decayed(i, k):
                t, h = k // 4, 4 * (k % 4)
                dve.wait_ge(ret_full, NRET * i + k + 1)
                if k == 0:
                    dve.wait_ge(oB_psum, i)
                dve.tensor_tensor(PR[:, t, h:h + 4, :], ring[k % 2][:, :].rearrange("p (h q) -> p h q", h=4),
                                  decay.unsqueeze(1).to_broadcast([P, 4, P]), ALU.mult).then_inc(ret_done, 1)

            def norm_of_r(i):
                dve.wait_ge(oBT_psum, i + 1)
                norm(norm_r, b_4[:, 0:S].rearrange("p (t d) -> p t d", t=T), zR, i)

            def gated_b(i):
                dve.wait_ge(nT_ready, i + 1)
                dve.wait_ge(gate_ready, i + 1)
                dve.scalar_tensor_tensor(out=yT[:, :], in0=gate[:, :], scalar=1.0, in1=nT[:, :], op0=ALU.add, op1=ALU.mult).then_inc(yT_ready, 1)

            def residual_b(i):
                dve.wait_ge(projB, i + 1)
                dve.wait_ge(x2_copied, 16 * (i + 1))
                dve.tensor_tensor(x3[:, :, :].rearrange("p t d -> p (t d)"), x2_res[:, :, :].rearrange("p t d -> p (t d)"),
                                  b_4[:, S:2 * S], ALU.add).then_inc(projB_used, 1)
                dve.wait_ge(projB_used, i + 1)
                norm(norm_f2, x3, f2.z, i)

            def x2_free(i):
                dve.wait_ge(x2_copied, 16 * i)

            def x4_free(i):
                dve.wait_ge(out_done, 16 * i)

            def slot(s):
                one, two, three, four = (running(s, n) for n in range(4))
                if one:
                    norm_of_a(s)
                if three:
                    norm_of_f1(s - 2)
                if one:
                    rope_products(s)
                if three:
                    ffn_mix(f1, s - 2)
                for k in range(NRET):
                    if four:
                        decayed(s - 3, k)
                    if k == 5 and three:
                        ffn_out(f1, s - 2, x2_free)
                if one:
                    rest_a(s)
                    last_a(s)
                if three:
                    norm_of_b(s - 2)
                if four:
                    norm_of_r(s - 3)
                if two:
                    normalise(s - 1)
                if three:
                    rest_b(s - 2)
                if four:
                    gated_b(s - 3)
                if two:
                    residual_a(s - 1)
                if four:
                    residual_b(s - 3)
                for k in range(NFILL):
                    if one:
                        row_max(s, k)
                    if k == 3 and three:
                        keep_heads(s - 2)
                    if k == 5 and four:
                        ffn_mix(f2, s - 3)
                if four:
                    ffn_out(f2, s - 3, x4_free)

            slots(dve, slot)

        @block.tensor
        def _(pe):
            def turn(dst, src, n=T):
                for t in range(n):
                    ins = pe.transpose(dst[:, t * P:(t + 1) * P], src[:, t, :], ident)
                return ins

            def add_bias(dst, first, width):
                return pe.matmul(dst, ones3[:, :], bias[:, first * D:first * D + width], start=False, stop=True, skip_group_check=True)

            pe.wait_ge(tables_in, 16 * 15)
            for n in range(3):
                ins = pe.transpose(b_3[:, n * D:(n + 1) * D], wf[:, n, :], ident)
            ins.then_inc(wf_turned, 1)
            pe.wait_ge(bias_rows_in, 16 * PARTS)
            pe.wait_ge(cleared, 11)
            pe.wait_ge(masks_ready, 1)
            pe.wait_ge(wf_ready, 1)

            def a_turn(i):
                pe.wait_ge(norm_a.done, i + 1)
                pe.wait_ge(maxT_ready, i)
                turn(b_1, zA).then_inc(zAT_psum, 1)

            def a_qk(i):
                pe.wait_ge(zAT_ready, i + 1)
                for t in range(T):
                    dst = b_1[:, t * QKW:(t + 1) * QKW]
                    pe.matmul(dst, zAT[:, t * P:(t + 1) * P], wa[:, 0:2, :].rearrange("p n d -> p (n d)"), start=True, stop=False, skip_group_check=True)
                    ins = add_bias(dst, 0, QKW)
                ins.then_inc(qkA_psum, 1)

            def a_turn_qk(i):
                pe.wait_ge(rotated, i + 1)
                for n in range(2):
                    for t in range(T):
                        ins = pe.transpose(b_1[:, n * S + t * P:n * S + (t + 1) * P], rot[:, t, n, :], ident)
                ins.then_inc(rotT_psum, 1)

            def a_v(i):
                pe.wait_ge(splitA, 3 * (i + 1))
                for t in range(T):
                    dst = b_1[:, t * D:(t + 1) * D]
                    pe.matmul(dst, zAT[:, t * P:(t + 1) * P], wa[:, 2, :], start=True, stop=False, skip_group_check=True)
                    ins = add_bias(dst, 2, D)
                ins.then_inc(vA_psum, 1)

            def score_fill(i, k, before):
                if k == 0:
                    pe.wait_ge(stackA_in, 16 * NSTACK * (i + 1))
                if k < 2:
                    before(k)
                else:
                    pe.wait_ge(scores_max, NFILL * i + k - 1)
                dst = ring[k % 2]
                if k < 4:
                    pe.matmul(dst[:, :], identb, future, start=True, stop=False, skip_group_check=True)
                    for n in range(4):
                        h = 4 * k + n
                        ins = pe.matmul(dst[:, n * P:(n + 1) * P], Qst[0:ROWS, h, 0:P], Kst[0:ROWS, h, 0:P], start=False, stop=True, skip_group_check=True)
                else:
                    pe.matmul(dst[:, :].rearrange("p (h k) -> p h k", h=2)[:, :, P:S], identb,
                              future[:, 0:2 * P].rearrange("p (h k) -> p h k", h=2), start=True, stop=False, skip_group_check=True)
                    for n in range(2):
                        h = 2 * (k - 4) + n
                        ins = pe.matmul(dst[:, n * S:(n + 1) * S], Qst[0:ROWS, h, P:S], Kst[0:ROWS, h, :], start=False, stop=True, skip_group_check=True)
                ins.then_inc(scores_full, 1)

            def a_turn_max(i):
                pe.wait_ge(maxp_ready, i + 1)
                pe.wait_ge(vA_ready, i + 1)
                apart(pe, "pe")
                dst = b_1[0:PARTS * H, 0:S // 2].bitcast(BF16)
                for t in range(T):
                    ins = pe.transpose(dst[:, t * P:(t + 1) * P], maxp[:, t, :, :].rearrange("p n h -> p (n h)"), identb)
                ins.then_inc(maxT_psum, 1)

            def exp_fill(i, g):
                if g == 0:
                    pe.wait_ge(max_rows_in, 16 * PARTS * (i + 1))
                if g >= 2:
                    pe.wait_ge(exp_done, NFILL * i + g - 1)
                elif not (isinstance(i, int) and i == 0):
                    pe.wait_ge(exp_done, NFILL * i)
                _, kt, h0 = EXP_FILLS[g]
                dst = exp_ring[g % 2]
                w = S if kt == 0 else P
                for n in range(512 // w):
                    h = h0 + n
                    ins = pe.matmul(dst[:, n * w:(n + 1) * w], Kst[0:XROWS, h, kt * P:(kt + 1) * P], Qst[0:XROWS, h, S - w:S], start=True, stop=True, skip_group_check=True)
                ins.then_inc(st_full, 1)

            def pv(i, half_):
                pe.wait_ge(masked, NFILL * i + 6 * (half_ + 1))
                if half_ == 0:
                    pe.wait_ge(vA_ready, i + 1)
                    pe.wait_ge(x1_ready, i)
                o = half_ * S
                for kt in range(T):
                    for n in range(2):
                        for j in range(NCT):
                            h = hs(half_, j, n)
                            rhs = P0[:, h, :] if kt == 0 else P1[:, h, :]
                            ins = pe.matmul(b_o[j * CT:(j + 1) * CT, o + kt * P:o + S], VA[:, kt, h, :], rhs,
                                            start=(half_ == 0 and kt == 0 and n == 0), stop=(kt == 1 and n == 1), skip_group_check=True)
                ins.then_inc(pv_done, 1)

            def o_turn(i):
                pe.wait_ge(oA_ready, i + 1)
                for t in range(T):
                    for half_ in range(2):
                        ins = pe.transpose(b_o[:, (2 * t + half_) * P:(2 * t + half_ + 1) * P], oA[:, half_ * S + t * P:half_ * S + (t + 1) * P], ident)
                ins.then_inc(oAT_psum, 1)

            def ctx_turn(i):
                pe.wait_ge(ctx_ready, i + 1)
                turn(b_o, ctxA).then_inc(ctxT_psum, 1)

            def a_out(i):
                pe.wait_ge(ctxT_ready, i + 1)
                for t in range(T):
                    dst = b_o[:, S + t * D:S + (t + 1) * D]
                    pe.matmul(dst, ctxT[:, t * P:(t + 1) * P], wa[:, 3, :], start=True, stop=False, skip_group_check=True)
                    ins = add_bias(dst, 3, D)
                ins.then_inc(projA, 1)

            def ffn_turn(F, i):
                pe.wait_ge(F.norm.done, i + 1)
                turn(F.psum, F.z).then_inc(F.turned, 1)

            def ffn_rk(F, i):
                pe.wait_ge(F.mixed, 2 * (i + 1))
                for t in range(T):
                    pe.matmul(F.psum[:, S + t * D:S + (t + 1) * D], F.mix[:, 0, t * P:(t + 1) * P], wfT[:, 0, :], start=True, stop=True)
                pe.matmul(F.psum[:, 0:S], wfT[:, 1, :], F.mix[:, 1, :], start=True, stop=True).then_inc(F.rk_ready, 1)

            def ffn_v(F, i):
                pe.wait_ge(F.squared, i + 1)
                pe.wait_ge(F.tanh_done, i + 1)
                for t in range(T):
                    ins = pe.matmul(F.psum[:, t * D:(t + 1) * D], F.ka[:, t * P:(t + 1) * P], wfT[:, 2, :], start=True, stop=True)
                ins.then_inc(F.v_ready, 1)

            def b_turn(i):
                pe.wait_ge(norm_b.done, i + 1)
                turn(b_3, zB).then_inc(zBT_psum, 1)

            def b_qk(i):
                pe.wait_ge(zBT_ready, i + 1)
                for n in range(2):
                    ins = pe.matmul(b_3[:, n * S:(n + 1) * S], wqk_dh[:, n, :], zBT[:, :], start=True, stop=True)
                ins.then_inc(qkB_psum, 1)

            def b_vg(i):
                pe.wait_ge(qkB_ready, 2 * (i + 1))
                for t in range(T):
                    dst = b_3[:, t * D:(t + 1) * D]
                    pe.matmul(dst, zBT[:, t * P:(t + 1) * P], wb[:, 2, :], start=True, stop=False, skip_group_check=True)
                    add_bias(dst, 4, D)
                pe.matmul(b_3[:, S:2 * S], wb[:, 3, :], zBT[:, :], start=True, stop=True).then_inc(vg_psum, 1)

            def b_kv(i):
                pe.wait_ge(vB_ready, i + 1)
                pe.wait_ge(gate_ready, i + 1)
                pe.transpose(b_3[:, 0:D], qkB[:, 1, 0:P], ident).then_inc(kB_psum, 1)
                pe.wait_ge(kdec_ready, i + 1)
                first = quad_view(VB)[:, 0:NCT, :, :]
                pe.matmul(b_3[:, D:2 * D], kdec[:, :], first, start=True, stop=True).then_inc(kv_psum, 1)

            def ret_fill(i, k, before):
                if k == 0:
                    pe.wait_ge(stackB_in, 16 * NSTACK * (i + 1))
                if k < 2:
                    before(k)
                else:
                    pe.wait_ge(ret_done, NRET * i + k - 1)
                t = k // 4
                for n in range(4):
                    h = 4 * (k % 4) + n
                    ins = pe.matmul(ring[k % 2][:, n * P:(n + 1) * P], Rk[:, h, t * P:(t + 1) * P], Rq[:, h, t * P:(t + 1) * P], start=True, stop=True, skip_group_check=True)
                ins.then_inc(ret_full, 1)

            def b_pv(i):
                pe.wait_ge(ret_done, NRET * (i + 1))
                pe.wait_ge(state_ready, i + 1)
                pe.wait_ge(qdec_ready, i + 1)
                pe.wait_ge(f2.x_ready, i)
                for t in range(T):
                    if t == 1:
                        pe.matmul(b_4[:, P:S], state[:, :], qdec[:, :], start=False, stop=False, skip_group_check=True)
                    for n in range(4):
                        for j in range(NCT):
                            h = 4 * j + n
                            ins = pe.matmul(b_4[j * CT:(j + 1) * CT, t * P:(t + 1) * P], VB[:, t, h, :], PR[:, t, h, :],
                                            start=(t == 0 and n == 0), stop=(n == 3), skip_group_check=True)
                ins.then_inc(oB_psum, 1)

            def b_turn_o(i):
                pe.wait_ge(oB_ready, i + 1)
                for t in range(T):
                    ins = pe.transpose(b_4[:, t * P:(t + 1) * P], oB[:, t * P:(t + 1) * P], ident)
                ins.then_inc(oBT_psum, 1)

            def b_turn_n(i):
                pe.wait_ge(norm_r.done, i + 1)
                turn(b_4, zR).then_inc(zRT_psum, 1)

            def b_out(i):
                pe.wait_ge(yT_ready, i + 1)
                for t in range(T):
                    dst = b_4[:, S + t * D:S + (t + 1) * D]
                    pe.matmul(dst, yT[:, t * P:(t + 1) * P], wb[:, 4, :], start=True, stop=False, skip_group_check=True)
                    ins = add_bias(dst, 5, D)
                ins.then_inc(projB, 1)

            def slot(s):
                one, two, three, four = (running(s, n) for n in range(4))
                done = min(s, B) if isinstance(s, int) else s

                def ring_after_scores(k):
                    pe.wait_ge(scores_max, NFILL * done)

                def ring_after_retention(k):
                    if four:
                        pe.wait_ge(ret_done, NRET * (s - 2))
                    else:
                        ring_after_scores(k)

                if one:
                    a_turn(s)
                if three:
                    ffn_turn(f1, s - 2)
                if one:
                    a_qk(s)
                if three:
                    ffn_rk(f1, s - 2)
                for g in range(NFILL):
                    if two:
                        exp_fill(s - 1, g)
                    if four and g < NRET:
                        ret_fill(s - 3, g, ring_after_scores)
                    if g == 5 and three:
                        ffn_v(f1, s - 2)
                    if g == 7 and one:
                        a_turn_qk(s)
                    if g == 10 and two:
                        pv(s - 1, 0)
                if four:
                    b_pv(s - 3)
                if three:
                    b_turn(s - 2)
                if two:
                    pv(s - 1, 1)
                if one:
                    a_v(s)
                if four:
                    b_turn_o(s - 3)
                if two:
                    o_turn(s - 1)
                if three:
                    b_qk(s - 2)
                if four:
                    b_turn_n(s - 3)
                if two:
                    ctx_turn(s - 1)
                    a_out(s - 1)
                if four:
                    b_out(s - 3)
                for k in range(NFILL):
                    if one:
                        score_fill(s, k, ring_after_retention)
                    if k == 2 and three:
                        b_vg(s - 2)
                    if k == 3 and four:
                        ffn_turn(f2, s - 3)
                    if k == 5 and three:
                        b_kv(s - 2)
                    if k == 7 and four:
                        ffn_rk(f2, s - 3)
                    if k == 9 and four:
                        ffn_v(f2, s - 3)
                if one:
                    a_turn_max(s)

            slots(pe, slot)


_OUT = ((B, S, D), "float32")
_A = ["Wq", "bq", "Wk", "bk", "Wv", "bv", "Wo", "bo"]
_B = ["Wq", "bq", "Wk", "bk", "Wv", "bv", "Wg", "bg", "Wo", "bo", "gamma", "beta"]
_F = ["W_r", "W_k", "W_v", "mu_r", "mu_k"]


def kernel(**inputs):
    import concourse.bacc as _bacc
    from concourse.bass_utils import run_bass_kernel_spmd as _run

    nc = _bacc.Bacc("TRN2", target_bir_lowering=False, num_devices=1)
    arrays = {}

    def given(name, value):
        v = np.ascontiguousarray(value)
        arrays[f"in_{name}"] = v
        return nc.dram_tensor(f"in_{name}", v.shape, mybir.dt.from_np(v.dtype), kind="ExternalInput").ap()

    x = given("x", inputs["L0_attn_a_x"])
    a = {n: given(f"a_{n}", inputs[f"L0_attn_a_{n}"]) for n in _A}
    b = {n: given(f"b_{n}", inputs[f"L0_attn_b_{n}"]) for n in _B}
    f = {n: given(f"f_{n}", inputs[f"L0_ffn_{n}"]) for n in _F}
    c = {n: given(n, v) for n, v in constants().items()}
    out = nc.dram_tensor("out", _OUT[0], mybir.dt.from_np(np.dtype(_OUT[1])), kind="ExternalOutput").ap()
    build(nc, x, a, b, f, c, out)
    r = _run(nc, [arrays], core_ids=[0])
    return r.results[0]["out"]
```

```python
from contextlib import ExitStack

import concourse.bass as bass
from concourse import mybir
import numpy as np

ALU = mybir.AluOpType
ACT = mybir.ActivationFunctionType
AX_X = mybir.AxisListType.X
F32 = mybir.dt.float32
BF16 = mybir.dt.bfloat16

B, S, D = 8, 256, 128
P = 128
T = S // P
H, HD = 16, 8
PARTS = 3
PAIRS = PARTS * PARTS
KPARTS = 2 * PARTS - 1
HALF = H // 2
ROWS = HD * PAIRS
XROWS = ROWS + PARTS
SLOT = HD + 1
CT = 32
NCT = P // CT
SCALE = float(HD) ** -0.5
DECAY = 0.99
EPS = 1e-5
BIG = 1e30
QKW = 2 * D
STAGES = 5
PSUM_USES = [
    ("b_turn_o", 0, 4), ("f1_v", 2, 3), ("a_turn", 1, 1), ("a_v", 2, 2), ("b_turn", 3, 3), ("turn_max0", 1, 2), ("b_qk", 3, 3),
    ("b_turn_n", 1, 4), ("a_qk", 0, 1), ("b_out", 1, 4), ("turn_max1", 3, 2), ("turn_k", 2, 3), ("b_vg", 0, 3), ("a_turn_qk", 1, 1),
    ("f2_turn", 2, 4), ("pv", 3, 2), ("f2_rk", 1, 4), ("b_kv", 1, 3), ("o_turn", 2, 2), ("ctx_turn", 0, 2), ("a_out", 3, 2),
    ("f2_v", 0, 4), ("b_pv", 3, 3), ("f1_turn", 2, 2), ("f1_rk", 0, 2),
]


def constants():
    freq = np.power(np.float32(10000.0), np.float32(-2.0) * np.arange(D // 2, dtype=np.float32) / np.float32(D))
    ang = (np.arange(S, dtype=np.float32)[:, None] * freq.astype(np.float32)[None, :]).astype(np.float32)
    cos, sin = np.cos(ang), np.sin(ang)

    def rope(first, second):
        t = np.concatenate([first, second], axis=1).reshape(T, P, 1, D)
        return np.repeat(t, 2, axis=2).transpose(1, 0, 2, 3).reshape(P, T * 2 * D).astype(np.float32)

    i = np.arange(P)
    same_head = (i[:, None] % H == i[None, :] // HD).astype(np.float32)
    from_middle = np.power(np.float64(DECAY), np.arange(S) - S // 2)
    qk_decay = np.tile(np.concatenate([from_middle * SCALE, 1.0 / from_middle])[None, :], (P, 1)).astype(np.float32)
    future = np.where(i[None, :] > i[:, None], -BIG, 0.0)
    return {
        "c_rope": np.concatenate([rope(cos, sin), rope(sin, cos)], axis=1),
        "c_f32": np.concatenate([np.eye(P, dtype=np.float32), same_head, qk_decay], axis=1),
        "c_bf16": np.concatenate([np.eye(P), np.tile(future, (1, 4))], axis=1).astype(np.float32),
    }


def build(nc, x, a, b, f, c, out):
    ctx = ExitStack()
    with ctx:
        def sb(name, shape, dt=F32):
            return ctx.enter_context(nc.sbuf_tensor(name, shape, dt))

        def sem(name):
            return ctx.enter_context(nc.semaphore(name))

        rope = sb("rope", [P, 2, T * QKW])
        cf = sb("cf", [P, 2 * P + 2 * S])
        cb = sb("cb", [P, P + 4 * P], BF16)
        ident, same_head, qk_decay = cf[:, 0:P], cf[:, P:2 * P], cf[:, 2 * P:]
        identb, future = cb[:, 0:P], cb[:, P:5 * P]
        wa = sb("wa", [P, 4, D])
        wb = sb("wb", [P, 5, D])
        wqk_dh = sb("wqk_dh", [P, 2, D])
        wf = sb("wf", [P, 3, D])
        wfT = sb("wfT", [P, 3, D])
        vecs = sb("vecs", [P, 7])
        half = sb("half", [P, 3])
        NB = 6
        brow = sb("brow", [1, 3, NB * D])
        browp = sb("browp", [1, PARTS, NB * D], BF16)
        bias = sb("bias", [PARTS, NB * D], BF16)
        minus_half = sb("minus_half", [P, T])
        ones3 = sb("ones3", [PARTS, P], BF16)

        x_in = sb("x_in", [P, T, D])
        zA = sb("zA", [P, T, D])
        zAT = sb("zAT", [P, S])
        prod = sb("prod", [P, 2, T * QKW])
        rot = sb("rot", [P, T, 2, D])
        partsA = sb("partsA", [P, PARTS, 2 * S], BF16)
        remA = sb("remA", [P, 2 * S])
        Qst = sb("Qst", [XROWS, H, S], BF16)
        Kst = sb("Kst", [XROWS, H, S], BF16)
        mx = sb("mx", [P, T, H])
        mrem = sb("mrem", [P, T, H])
        maxp = sb("maxp", [P, T, 2, PARTS, HALF], BF16)
        maxT = sb("maxT", [PARTS * HALF, 2, S], BF16)
        VA = sb("VA", [P, T, H, CT])
        x_res = sb("x_res", [P, T, D])
        P0 = sb("P0", [P, H, S])
        P1 = sb("P1", [P, H, P])
        oA = sb("oA", [P, 2 * S])
        rsum = sb("rsum", [P, T * H // 2, 2])
        ctxA = sb("ctxA", [P, T, D])
        ctxT = sb("ctxT", [P, S])
        x1 = sb("x1", [P, T, D])
        x2 = sb("x2", [P, T, D])
        zB = sb("zB", [P, T, D])
        zBT = sb("zBT", [P, S])
        qkB = sb("qkB", [P, 2, S])
        qkS = sb("qkS", [P, 2, S])
        partsB = sb("partsB", [P, PARTS, 2 * S], BF16)
        remB = sb("remB", [P, 2 * S])
        Rq = sb("Rq", [ROWS, H, S], BF16)
        Rk = sb("Rk", [ROWS, H, S], BF16)
        VB = sb("VB", [P, T, H, CT])
        gate = sb("gate", [P, S])
        kdec = sb("kdec", [P, D])
        state = sb("state", [P, D])
        x2_res = sb("x2_res", [P, T, D])
        PR = sb("PR", [P, T, H, P])
        oB = sb("oB", [P, S])
        zR = sb("zR", [P, T, D])
        nT = sb("nT", [P, S])
        yT = sb("yT", [P, S])
        x3 = sb("x3", [P, T, D])
        x4 = sb("x4", [P, T, D])

        bank = [ctx.enter_context(nc.psum_tensor(f"bank{n}", [P, 512], F32)) for n in range(8)]
        ring = bank[0:2]
        exp_ring = bank[2:4]
        psum = {name: bank[4 + n] for name, n, _ in PSUM_USES}

        class Norm:
            def __init__(self, name):
                self.st = sb(f"{name}_st", [P, T, 6])
                self.mv = sb(f"{name}_mv", [P, T, 2])
                self.var = sb(f"{name}_var", [P, T])
                self.rstd = sb(f"{name}_rstd", [P, T])
                self.stats, self.moments, self.shifted, self.rdev, self.done = (
                    sem(f"{name}_{n}") for n in ("stats", "moments", "shifted", "rdev", "done"))

        norm_a, norm_f1, norm_b, norm_r, norm_f2 = (Norm(n) for n in ("norm_a", "norm_f1", "norm_b", "norm_r", "norm_f2"))

        class Ffn:
            def __init__(self, name, norm, src, dst):
                self.name, self.norm, self.src, self.dst = name, norm, src, dst
                self.z = sb(f"{name}_z", [P, T, D])
                self.zT = sb(f"{name}_zT", [P, 1 + S])
                self.dz = sb(f"{name}_dz", [P, S])
                self.mix = sb(f"{name}_mix", [P, 2, S])
                self.kr = sb(f"{name}_kr", [P, S])
                self.ka = sb(f"{name}_ka", [P, S])
                self.th = sb(f"{name}_th", [P, T, D])
                self.u = sb(f"{name}_u", [P, T, D])
                self.turned = sem(f"{name}_turned")
                self.zT_ready = sem(f"{name}_zT_ready")
                self.dz_ready = sem(f"{name}_dz_ready")
                self.mixed = sem(f"{name}_mixed")
                self.rk_ready = sem(f"{name}_rk_ready")
                self.relu_done = sem(f"{name}_relu_done")
                self.tanh_done = sem(f"{name}_tanh_done")
                self.squared = sem(f"{name}_squared")
                self.v_ready = sem(f"{name}_v_ready")
                self.gated = sem(f"{name}_gated")
                self.x_ready = sem(f"{name}_x_ready")

        f1 = Ffn("f1", norm_f1, x1, x2)
        f2 = Ffn("f2", norm_f2, x3, x4)

        tables_in, biases_in, bias_rows_in, wf_in = sem("tables_in"), sem("biases_in"), sem("bias_rows_in"), sem("wf_in")
        masks_ready = sem("masks_ready")
        bias_split, cleared, wf_turned, wf_ready, halved = (sem(n) for n in ("bias_split", "cleared", "wf_turned", "wf_ready", "halved"))
        xin_in, zAT_psum, zAT_ready, qkA_psum, products, rotated = (
            sem(n) for n in ("xin_in", "zAT_psum", "zAT_ready", "qkA_psum", "products", "rotated"))
        rotT_psum, splitA, splitA_rem, vA_psum, vA_ready = (
            sem(n) for n in ("rotT_psum", "splitA", "splitA_rem", "vA_psum", "vA_ready"))
        stackA_in, max_rows_in = ([sem(f"{n}_{half_}") for half_ in range(2)] for n in ("stackA_in", "max_rows_in"))
        scores_full, scores_max, maxp_step, maxp_ready, maxT_psum, maxT_ready = (
            sem(n) for n in ("scores_full", "scores_max", "maxp_step", "maxp_ready", "maxT_psum", "maxT_ready"))
        st_full, exp_done, masked, pv_done, oA_ready, oAT_psum, rsum_ready, ctx_ready, ctxT_psum, ctxT_ready, projA, x1_ready = (
            sem(n) for n in ("st_full", "exp_done", "masked", "pv_done", "oA_ready", "oAT_psum", "rsum_ready", "ctx_ready",
                             "ctxT_psum", "ctxT_ready", "projA", "x1_ready"))
        xres_in, zBT_psum, zBT_ready, qkB_psum, qkB_ready, splitB, splitB_rem, stackB_in = (
            sem(n) for n in ("xres_in", "zBT_psum", "zBT_ready", "qkB_psum", "qkB_ready", "splitB", "splitB_rem", "stackB_in"))
        vg_psum, vB_ready, gate_ready, kB_psum, kdec_ready, qkS_ready, kv_psum, state_ready, x2_copied = (
            sem(n) for n in ("vg_psum", "vB_ready", "gate_ready", "kB_psum", "kdec_ready", "qkS_ready", "kv_psum", "state_ready", "x2_copied"))
        ret_full, ret_copied, ret_done, oB_psum, oB_ready, oBT_psum, zRT_psum, nT_ready, yT_ready, projB, out_done = (
            sem(n) for n in ("ret_full", "ret_copied", "ret_done", "oB_psum", "oB_ready", "oBT_psum", "zRT_psum", "nT_ready", "yT_ready", "projB", "out_done"))

        NFILL = T * H * P * T // 512 - H * P // 512
        NRET = T * H * P // 512
        NSTACK = 2
        NSPILL = 3

        def running(s, stage):
            return not isinstance(s, int) or 0 <= s - stage < B

        passed = {e: sem(f"passed_{e}") for e in ("pe", "dve", "pool", "sp")}

        def apart(eng, name):
            eng.sem_inc(passed[name], 1)

        def slots(eng, body):
            for s in range(STAGES):
                body(s)
            with eng.Fori(STAGES, B) as s:
                body(s)
            for s in range(B, B + STAGES - 1):
                body(s)

        def hs(set_, j, n):
            return set_ * 8 + 2 * j + n

        SCORE_FILLS = [(t, h, n) for half_ in range(2) for t, n in ((0, 4), (1, 2)) for h in range(8 * half_, 8 * half_ + 8, n)]
        EXP_FILLS = [(half_, kt, h) for half_ in range(2) for kt, n in ((0, 2), (1, 4)) for h in range(8 * half_, 8 * half_ + 8, n)]

        scratchA, scratchB = ([nc.dram_tensor(f"parts_{w}_{n}", (parts, D, S), BF16, kind="Internal").ap()
                               for n, parts in (("q", PARTS), ("k", KPARTS))] for w in "ab")
        spilledA, spilledB, projB_used = sem("spilledA"), sem("spilledB"), sem("projB_used")

        block = ctx.enter_context(nc.Block())

        def pair_view(v):
            whole = v[:, :, :, :]
            return bass.AP(whole.tensor, whole.offset, [whole.ap[0], [2 * CT, T * H // 2], [CT + SLOT, 2], [1, HD]])

        def quad_view(v):
            whole = v[:, :, :, :]
            return bass.AP(whole.tensor, whole.offset, [whole.ap[0], [4 * CT, T * H // 4], [CT + HD, 4], [1, HD]])

        @block.sync
        def _(sp):
            sp.dma_start(rope[:, :, :], c["c_rope"].rearrange("p (a n) -> p a n", a=2)).then_inc(tables_in, 16)
            sp.dma_start(cf[:, :], c["c_f32"]).then_inc(tables_in, 16)
            sp.dma_start(prod[:, :, :].rearrange("p a n -> p (a n)")[:, 0:5 * P], c["c_bf16"]).then_inc(tables_in, 16)
            for n, w in enumerate((a["Wq"], a["Wk"], a["Wv"], a["Wo"])):
                sp.dma_start(wa[:, n, :], w).then_inc(tables_in, 16)
            for n, w in enumerate((b["Wq"], b["Wk"], b["Wv"], b["Wg"], b["Wo"])):
                sp.dma_start(wb[:, n, :], w).then_inc(tables_in, 16)
            for n, w in enumerate((f["W_r"], f["W_k"], f["W_v"])):
                sp.dma_start(wf[:, n, :], w).then_inc(tables_in, 16)
            for n, w in enumerate((a["bq"], a["bk"], a["bv"], a["bo"], b["bv"], b["bo"])):
                sp.dma_start(brow[0:1, 0, n * D:(n + 1) * D], w.rearrange("(o n) -> o n", o=1)).then_inc(biases_in, 16)
            with nc.allow_non_contiguous_dma(reason="seven vectors onto partitions, once"):
                for n, w in enumerate((f["mu_r"], f["mu_k"], b["bg"], b["gamma"], b["beta"])):
                    sp.dma_start(vecs[:, n:n + 1], w.rearrange("(n o) -> n o", o=1)).then_inc(biases_in, 16)
                for n, w in enumerate((b["bq"], b["bk"])):
                    sp.dma_start(vecs[:, 5 + n:6 + n], bass.AP(w.tensor, w.offset, [[1, HD], [HD, H], [1, 1]])).then_inc(biases_in, 16)
            sp.wait_ge(bias_split, 5)
            for n in range(PARTS):
                sp.dma_start(bias[n:n + 1, :], browp[0:1, n, :]).then_inc(bias_rows_in, 16)

            def load_x(i):
                if not (isinstance(i, int) and i == 0):
                    sp.wait_ge(norm_a.done, i)
                sp.dma_start(x_in[:, :, :], x[i].rearrange("(t p) d -> p t d", p=P)).then_inc(xin_in, 16)

            def load_x_res(i):
                sp.wait_ge(x1_ready, i)
                sp.dma_start(x_res[:, :, :], x[i].rearrange("(t p) d -> p t d", p=P)).then_inc(xres_in, 16)

            def spill_k_again(parts, k_scratch, spilled):
                sp.dma_start(k_scratch[PARTS:KPARTS].rearrange("m r t -> r m t"), parts[:, 0:PARTS - 1, S:2 * S]).then_inc(spilled, 16)

            def spill(parts, scratch, spilled):
                for n in range(2):
                    sp.dma_start(scratch[n][0:PARTS].rearrange("m r t -> r m t"), parts[:, :, n * S:(n + 1) * S]).then_inc(spilled, 16)

            def stacks(q_st, k_st, scratch, heads, landed):
                rows, run = PARTS * HD, (heads.stop - heads.start) * S
                for st, part, step in ((k_st, scratch[1], D * S), (q_st, scratch[0], 0)):
                    src = bass.AP(part.tensor, part.offset + heads.start * S, [[step, PARTS], [H * S, rows], [1, run]])
                    sp.dma_start(st[0:ROWS, heads, :], src).then_inc(landed, 16)

            def max_rows(i, half_):
                sp.wait_ge(maxT_ready, 2 * i + half_ + 1)
                sp.dma_start(Qst[ROWS:XROWS, half_ * HALF:(half_ + 1) * HALF, :],
                             maxT[:, half_, :]).then_inc(max_rows_in[half_], 16)

            def copy_x2(i):
                sp.wait_ge(projB_used, i)
                apart(sp, "sp")
                sp.wait_ge(f1.x_ready, i + 1)
                sp.dma_start(x2_res[:, :, :], x2[:, :, :]).then_inc(x2_copied, 16)

            def spill_b_early(i):
                sp.wait_ge(splitB, 3 * i + 2)
                spill_k_again(partsB, scratchB[1], spilledB)

            def spill_b(i):
                sp.wait_ge(splitB, 3 * i + 3)
                spill(partsB, scratchB, spilledB)

            def stack_b(i):
                sp.wait_ge(ret_full, NRET * i)
                apart(sp, "sp")
                sp.wait_ge(spilledB, 16 * NSPILL * (i + 1))
                stacks(Rq, Rk, scratchB, slice(0, H), stackB_in)

            def spill_a_early(i):
                sp.wait_ge(splitA, 3 * i + 2)
                spill_k_again(partsA, scratchA[1], spilledA)

            def spill_a(i):
                sp.wait_ge(splitA, 3 * i + 3)
                spill(partsA, scratchA, spilledA)

            def stack_a(i, half_):
                if not (isinstance(i, int) and i == 0):
                    sp.wait_ge(st_full, NFILL * (i - 1) + 6 * (half_ + 1))
                    apart(sp, "sp")
                sp.wait_ge(spilledA, 16 * NSPILL * (i + 1))
                stacks(Qst, Kst, scratchA, slice(half_ * HALF, (half_ + 1) * HALF), stackA_in[half_])

            def store(i):
                sp.wait_ge(f2.x_ready, i + 1)
                sp.dma_start(out[i].rearrange("(t p) d -> p t d", p=P), x4[:, :, :]).then_inc(out_done, 16)

            def slot(s):
                one, two, three, four, five = (running(s, n) for n in range(5))
                if three:
                    max_rows(s - 2, 0)
                    load_x_res(s - 2)
                if one:
                    load_x(s)
                if three:
                    max_rows(s - 2, 1)
                if four:
                    spill_b_early(s - 3)
                    spill_b(s - 3)
                    stack_b(s - 3)
                if two:
                    spill_a_early(s - 1)
                    spill_a(s - 1)
                    stack_a(s - 1, 0)
                if five:
                    store(s - 4)
                if two:
                    stack_a(s - 1, 1)
                if four:
                    copy_x2(s - 3)

            slots(sp, slot)
            sp.wait_ge(out_done, 16 * B)

        @block.gpsimd
        def _(pool):
            pool.memset(VA[:, :, :, :], 0.0).then_inc(cleared, 1)
            pool.memset(VB[:, :, :, :], 0.0).then_inc(cleared, 1)
            pool.memset(ones3[:, :], 1.0).then_inc(cleared, 1)
            pool.wait_ge(cleared, 3)
            pool.memset(Kst[64:XROWS, :, :], -1.0).then_inc(cleared, 1)
            pool.wait_ge(cleared, 4)
            pool.memset(f1.zT[:, 0:1], 0.0).then_inc(cleared, 1)
            pool.memset(f2.zT[:, 0:1], 0.0).then_inc(cleared, 1)
            pool.memset(minus_half[:, :], -0.5).then_inc(cleared, 1)
            pool.wait_ge(cleared, 7)
            va = VA[:, :, :, :].rearrange("p t (g n) c -> p (t g) n c", n=2)
            for n in range(2):
                pool.memset(va[:, :, n, n * SLOT + HD:n * SLOT + HD + 1], 1.0).then_inc(cleared, 1)
            pool.wait_ge(tables_in, 16 * 15)
            for n in range(2):
                pool.tensor_copy(wqk_dh[:, n, :].rearrange("c (d h) -> c h d", h=H), wb[:, n, :].rearrange("c (h d) -> c h d", d=HD)).then_inc(cleared, 1)

            def deviation(N, i):
                pool.wait_ge(N.moments, i + 1)
                apart(pool, "pool")
                pool.tensor_scalar(N.var[:, :], N.mv[:, :, 1], EPS, None, ALU.add).then_inc(N.shifted, 1)
                pool.wait_ge(N.shifted, i + 1)
                pool.wait_ge(N.done, i)
                pool.tensor_tensor(N.rstd[:, :], N.var[:, :], minus_half[:, :], ALU.pow).then_inc(N.rdev, 1)

            def rotate(i):
                pool.wait_ge(products, 2 * (i + 1))
                pool.wait_ge(rotT_psum, i)
                turned = rot[:, :, :, :].rearrange("p t w (d h) -> p (t w) h d", h=H)
                first, second = (prod[:, n, :].rearrange("p (w h d) -> p w h d", w=2 * T, d=HD) for n in range(2))
                pool.tensor_tensor(turned, first, second, ALU.subtract).then_inc(rotated, 1)

            def split_max(i, half_):
                step, heads = 6 * i + 3 * half_, slice(half_ * HALF, (half_ + 1) * HALF)
                pool.wait_ge(scores_max, NFILL * i + 6 * (half_ + 1))
                pool.wait_ge(maxT_psum, 2 * i)
                apart(pool, "pool")
                pool.tensor_copy(maxp[:, :, half_, 0, :], mx[:, :, heads]).then_inc(maxp_step, 1)
                pool.wait_ge(maxp_step, step + 1)
                pool.tensor_tensor(mrem[:, :, heads], mx[:, :, heads], maxp[:, :, half_, 0, :], ALU.subtract).then_inc(maxp_step, 1)
                pool.wait_ge(maxp_step, step + 2)
                apart(pool, "pool")
                pool.tensor_copy(maxp[:, :, half_, 1, :], mrem[:, :, heads]).then_inc(maxp_step, 1)
                pool.wait_ge(maxp_step, step + 3)
                pool.tensor_tensor(maxp[:, :, half_, 2, :], mrem[:, :, heads], maxp[:, :, half_, 1, :], ALU.subtract).then_inc(maxp_ready, 1)

            def mask(i, g):
                _, kt, h = EXP_FILLS[g]
                pool.wait_ge(exp_done, NFILL * i + g + 1)
                apart(pool, "pool")
                blockp = P0[:, h:h + 2, 0:P] if kt == 0 else P1[:, h:h + 4, :]
                pool.affine_select(out=blockp, in_=blockp, compare_op=ALU.is_ge, fill=0.0, base=0,
                                   pattern=[[0, blockp.shape[1]], [1, P]], channel_multiplier=-1).then_inc(masked, 1)

            def square(F, i):
                pool.wait_ge(F.relu_done, i + 1)
                pool.tensor_tensor(F.ka[:, :], F.kr[:, :], F.kr[:, :], ALU.mult).then_inc(F.squared, 1)

            def decay_qk(i):
                pool.wait_ge(qkB_ready, 2 * (i + 1))
                pool.wait_ge(oB_psum, i)
                pool.tensor_tensor(qkS[:, :, :].rearrange("p n s -> p (n s)"), qkB[:, :, :].rearrange("p n s -> p (n s)"), qk_decay, ALU.mult).then_inc(qkS_ready, 1)

            def ret_mask(i, k):
                pool.wait_ge(ret_copied, NRET * i + k + 1)
                apart(pool, "pool")
                t, h = k // 4, 4 * (k % 4)
                pool.affine_select(out=PR[:, t, h:h + 4, :], in_=PR[:, t, h:h + 4, :], compare_op=ALU.is_ge, fill=0.0, base=0,
                                   pattern=[[0, 4], [1, P]], channel_multiplier=-1).then_inc(ret_done, 1)

            def ret_masks(i, first, last):
                for k in range(first, last):
                    ret_mask(i, k)

            def masks(i, first, last):
                for g in range(first, last):
                    mask(i, g)

            def slot(s):
                one, two, three, four, five = (running(s, n) for n in range(5))
                if five:
                    ret_masks(s - 4, 2, 6)
                if four:
                    deviation(norm_f1, s - 3)
                if five:
                    ret_masks(s - 4, 6, 8)
                if four:
                    square(f1, s - 3)
                if five:
                    deviation(norm_r, s - 4)
                if four:
                    deviation(norm_b, s - 3)
                if three:
                    split_max(s - 2, 0)
                if four:
                    decay_qk(s - 3)
                if three:
                    split_max(s - 2, 1)
                if two:
                    rotate(s - 1)
                if three:
                    masks(s - 2, 0, 1)
                if five:
                    deviation(norm_f2, s - 4)
                if three:
                    masks(s - 2, 1, 12)
                if one:
                    deviation(norm_a, s)
                if five:
                    square(f2, s - 4)
                if four:
                    ret_masks(s - 3, 0, 2)

            slots(pool, slot)

        @block.scalar
        def _(act):
            act.wait_ge(biases_in, 16 * (NB + 5 + 2))
            act.mul(half[:, :], vecs[:, 2:5], 0.5).then_inc(halved, 1)
            act.wait_ge(wf_turned, 1)
            act.activation(wfT[:, :, :].rearrange("p a n -> p (a n)"), bank[0][:, 0:3 * D], ACT.Copy).then_inc(wf_ready, 1)
            act.wait_ge(halved, 1)
            act.wait_ge(cleared, 9)

            def norm_turn(i):
                act.wait_ge(zAT_psum, i + 1)
                act.wait_ge(vA_psum, i)
                act.activation(zAT[:, :], psum["a_turn"][:, 0:S], ACT.Copy).then_inc(zAT_ready, 1)

            def split_a(i):
                act.wait_ge(rotT_psum, i + 1)
                for half_ in range(2):
                    act.wait_ge(stackA_in[half_], 16 * NSTACK * i)
                act.activation(partsA[:, 0, :], psum["a_turn_qk"][:, :], ACT.Copy).then_inc(splitA, 1)

            def split_a_2(i):
                act.wait_ge(splitA_rem, i + 1)
                act.activation(partsA[:, 1, :], remA[:, :], ACT.Copy).then_inc(splitA, 1)

            def v_a(i):
                act.wait_ge(vA_psum, i + 1)
                act.wait_ge(pv_done, 2 * i)
                act.activation(pair_view(VA), psum["a_v"][:, 0:T * D].rearrange("p (g n d) -> p g n d", n=2, d=HD), ACT.Copy).then_inc(vA_ready, 1)

            def max_turn(i, half_):
                act.wait_ge(maxT_psum, 2 * i + half_ + 1)
                act.wait_ge(max_rows_in[half_], 16 * i)
                act.activation(maxT[:, half_, :], psum[f"turn_max{half_}"][0:PARTS * HALF, half_ * P:(half_ + 1) * P].bitcast(BF16), ACT.Copy).then_inc(maxT_ready, 1)

            def exponential(i, g):
                _, kt, h = EXP_FILLS[g]
                act.wait_ge(st_full, NFILL * i + g + 1)
                if g == 0:
                    act.wait_ge(pv_done, 2 * i)
                dst = P0[:, h:h + 2, :] if kt == 0 else P1[:, h:h + 4, :]
                act.activation(dst.rearrange("p h q -> p (h q)"), exp_ring[g % 2][:, :], ACT.Exp, scale=SCALE).then_inc(exp_done, 1)

            def o_a(i):
                act.wait_ge(pv_done, 2 * (i + 1))
                act.wait_ge(oAT_psum, i)
                act.activation(oA[:, :], psum["pv"][:, :], ACT.Copy).then_inc(oA_ready, 1)

            def ctx_turn(i):
                act.wait_ge(ctxT_psum, i + 1)
                act.wait_ge(projA, i)
                act.activation(ctxT[:, :], psum["ctx_turn"][:, 0:S], ACT.Copy).then_inc(ctxT_ready, 1)

            def ffn_zT(F, i):
                act.wait_ge(F.turned, i + 1)
                act.activation(F.zT[:, 1:1 + S], psum[F.name + "_turn"][:, 0:S], ACT.Copy).then_inc(F.zT_ready, 1)

            def ffn_act(F, i):
                act.wait_ge(F.rk_ready, i + 1)
                act.activation(F.kr[:, :], psum[F.name + "_rk"][:, 0:S], ACT.Relu).then_inc(F.relu_done, 1)
                act.activation(F.th[:, :, :].rearrange("p t d -> p (t d)"), psum[F.name + "_rk"][:, S:2 * S], ACT.Tanh, scale=0.5).then_inc(F.tanh_done, 1)

            def b_turn(i):
                act.wait_ge(zBT_psum, i + 1)
                act.wait_ge(vg_psum, i)
                act.activation(zBT[:, :], psum["b_turn"][:, 0:S], ACT.Copy).then_inc(zBT_ready, 1)

            def b_qk(i):
                act.wait_ge(qkB_psum, i + 1)
                act.wait_ge(qkS_ready, i)
                for n in range(2):
                    act.activation(qkB[:, n, :], psum["b_qk"][:, n * S:(n + 1) * S], ACT.Identity, bias=vecs[:, 5 + n:6 + n]).then_inc(qkB_ready, 1)

            def split_b(i):
                act.wait_ge(qkS_ready, i + 1)
                act.wait_ge(stackB_in, 16 * NSTACK * i)
                act.activation(partsB[:, 0, :], qkS[:, :, :].rearrange("p n s -> p (n s)"), ACT.Copy).then_inc(splitB, 1)

            def split_b_2(i):
                act.wait_ge(splitB_rem, i + 1)
                act.activation(partsB[:, 1, :], remB[:, :], ACT.Copy).then_inc(splitB, 1)

            def b_vg(i):
                act.wait_ge(vg_psum, i + 1)
                act.wait_ge(oB_psum, i)
                act.activation(quad_view(VB), psum["b_vg"][:, 0:T * D].rearrange("p (g n d) -> p g n d", n=4, d=HD), ACT.Copy).then_inc(vB_ready, 1)
                act.wait_ge(yT_ready, i)
                act.activation(gate[:, :], psum["b_vg"][:, S:2 * S], ACT.Tanh, bias=half[:, 0:1], scale=0.5).then_inc(gate_ready, 1)

            def b_k(i):
                act.wait_ge(kB_psum, i + 1)
                act.activation(kdec[:, :], psum["turn_k"][:, 0:D], ACT.Copy).then_inc(kdec_ready, 1)

            def o_b(i):
                act.wait_ge(oB_psum, i + 1)
                act.wait_ge(oBT_psum, i)
                act.activation(oB[:, :], psum["b_pv"][:, 0:S], ACT.Copy).then_inc(oB_ready, 1)

            def affine_b(i):
                act.wait_ge(zRT_psum, i + 1)
                act.wait_ge(yT_ready, i)
                act.activation(nT[:, :], psum["b_turn_n"][:, 0:S], ACT.Identity, bias=half[:, 2:3], scale=half[:, 1:2]).then_inc(nT_ready, 1)

            def ret_copy(i, k):
                act.wait_ge(ret_full, NRET * i + k + 1)
                if k == 0:
                    act.wait_ge(oB_psum, i)
                t, h = k // 4, 4 * (k % 4)
                act.activation(PR[:, t, h:h + 4, :].rearrange("p h q -> p (h q)"), ring[k % 2][:, :], ACT.Copy).then_inc(ret_copied, 1)

            def exps(i, first, last):
                for g in range(first, last):
                    exponential(i, g)

            def ret_copies(i, first, last):
                for k in range(first, last):
                    ret_copy(i, k)

            def slot(s):
                one, two, three, four, five = (running(s, n) for n in range(5))
                if four:
                    o_a(s - 3)
                if five:
                    ret_copies(s - 4, 0, 4)
                if four:
                    ctx_turn(s - 3)
                if five:
                    ret_copies(s - 4, 4, 8)
                if four:
                    ffn_zT(f1, s - 3)
                if five:
                    o_b(s - 4)
                if four:
                    ffn_act(f1, s - 3)
                if two:
                    norm_turn(s - 1)
                if four:
                    b_turn(s - 3)
                if three:
                    max_turn(s - 2, 0)
                if four:
                    b_qk(s - 3)
                if five:
                    affine_b(s - 4)
                if three:
                    v_a(s - 2)
                    exps(s - 2, 0, 1)
                if four:
                    split_b(s - 3)
                if three:
                    max_turn(s - 2, 1)
                    exps(s - 2, 1, 3)
                if four:
                    split_b_2(s - 3)
                if three:
                    exps(s - 2, 3, 4)
                if four:
                    b_k(s - 3)
                if three:
                    exps(s - 2, 4, 6)
                if two:
                    split_a(s - 1)
                if three:
                    exps(s - 2, 6, 7)
                if five:
                    ffn_zT(f2, s - 4)
                if three:
                    exps(s - 2, 7, 12)
                if four:
                    b_vg(s - 3)
                if two:
                    split_a_2(s - 1)
                if five:
                    ffn_act(f2, s - 4)

            slots(act, slot)

        @block.vector
        def _(dve):
            def stats(N, src, i):
                for t in range(T):
                    ins = dve.bn_stats(N.st[:, t, :], src[:, t, :])
                ins.then_inc(N.stats, 1)
                dve.wait_ge(N.stats, i + 1)
                apart(dve, "dve")
                for t in range(T):
                    ins = dve.bn_aggr(N.mv[:, t, :], N.st[:, t, :])
                ins.then_inc(N.moments, 1)

            def apply(N, src, z, i, turned=None):
                dve.wait_ge(N.rdev, i + 1)
                if turned is not None:
                    dve.wait_ge(turned, i)
                for t in range(T):
                    ins = dve.tensor_scalar(z[:, t, :], src[:, t, :], N.mv[:, t, 0:1], N.rstd[:, t:t + 1], ALU.subtract, ALU.mult)
                ins.then_inc(N.done, 1)

            dve.wait_ge(biases_in, 16 * (NB + 5 + 2))
            dve.tensor_copy(browp[0:1, 0, :], brow[0:1, 0, :]).then_inc(bias_split, 1)
            for n in range(PARTS - 1):
                dve.wait_ge(bias_split, 2 * n + 1)
                dve.tensor_tensor(brow[0:1, n + 1, :], brow[0:1, n, :], browp[0:1, n, :], ALU.subtract).then_inc(bias_split, 1)
                dve.wait_ge(bias_split, 2 * n + 2)
                dve.tensor_copy(browp[0:1, n + 1, :], brow[0:1, n + 1, :]).then_inc(bias_split, 1)
            dve.wait_ge(tables_in, 16 * 15)
            dve.tensor_copy(cb[:, :], prod[:, :, :].rearrange("p a n -> p (a n)")[:, 0:5 * P]).then_inc(masks_ready, 1)

            def stats_a(i):
                dve.wait_ge(xin_in, 16 * (i + 1))
                stats(norm_a, x_in, i)

            def apply_a(i):
                apply(norm_a, x_in, zA, i, zAT_psum)

            def rope_products(i):
                dve.wait_ge(qkA_psum, i + 1)
                dve.wait_ge(rotated, i)
                qk = psum["a_qk"][:, :].rearrange("p (w f e) -> p w f e", w=2 * T, e=2)
                for n in range(2):
                    src = qk[:, :, :, n].unsqueeze(2).to_broadcast([P, 2 * T, 2, D // 2])
                    dve.tensor_tensor(prod[:, n, :].rearrange("p (w c f) -> p w c f", w=2 * T, c=2), src,
                                      rope[:, n, :].rearrange("p (w c f) -> p w c f", w=2 * T, c=2), ALU.mult).then_inc(products, 1)

            def rest_a(i):
                dve.wait_ge(splitA, 3 * i + 1)
                dve.tensor_tensor(remA[:, :], psum["a_turn_qk"][:, :], partsA[:, 0, :], ALU.subtract).then_inc(splitA_rem, 1)

            def last_a(i):
                dve.wait_ge(splitA, 3 * i + 2)
                dve.wait_ge(splitA_rem, i + 1)
                dve.tensor_tensor(partsA[:, 2, :], remA[:, :], partsA[:, 1, :], ALU.subtract).then_inc(splitA, 1)

            def row_max(i, k):
                dve.wait_ge(scores_full, NFILL * i + k + 1)
                if k == 0:
                    dve.wait_ge(maxp_ready, 2 * i)
                t, h, n = SCORE_FILLS[k]
                dve.tensor_reduce(mx[:, t, h:h + n], ring[k % 2][:, :].rearrange("p (h k) -> p h k", h=n), AX_X, ALU.max).then_inc(scores_max, 1)

            def normalise(i):
                dve.wait_ge(oAT_psum, i + 1)
                whole = psum["o_turn"][:, :]
                sums = bass.AP(whole.tensor, whole.offset + HD, [whole.ap[0], [CT, T * H // 2], [SLOT, 2]])
                vals = bass.AP(whole.tensor, whole.offset, [whole.ap[0], [CT, T * H // 2], [SLOT, 2], [1, HD]])
                dve.reciprocal(rsum[:, :, :], sums).then_inc(rsum_ready, 1)
                dve.wait_ge(rsum_ready, i + 1)
                dve.wait_ge(ctxT_psum, i)
                dve.tensor_tensor(ctxA[:, :, :].rearrange("p t (g n d) -> p (t g) n d", n=2, d=HD), vals,
                                  rsum[:, :, :].unsqueeze(3).to_broadcast([P, T * H // 2, 2, HD]), ALU.mult).then_inc(ctx_ready, 1)

            def residual_a(i):
                dve.wait_ge(projA, i + 1)
                dve.wait_ge(xres_in, 16 * (i + 1))
                dve.wait_ge(f1.x_ready, i)
                dve.tensor_tensor(x1[:, :, :].rearrange("p t d -> p (t d)"), x_res[:, :, :].rearrange("p t d -> p (t d)"),
                                  psum["a_out"][:, S:2 * S], ALU.add).then_inc(x1_ready, 1)

            def ffn_mix(F, i):
                dve.wait_ge(F.zT_ready, i + 1)
                now, before = F.zT[:, 1:1 + S], F.zT[:, 0:S]
                dve.tensor_tensor(F.dz[:, :], now, before, ALU.subtract).then_inc(F.dz_ready, 1)
                dve.wait_ge(F.dz_ready, i + 1)
                for n in range(2):
                    dve.scalar_tensor_tensor(out=F.mix[:, n, :], in0=F.dz[:, :], scalar=vecs[:, n:n + 1], in1=before,
                                             op0=ALU.mult, op1=ALU.add).then_inc(F.mixed, 1)

            def ffn_out(F, i, free):
                dve.wait_ge(F.v_ready, i + 1)
                dve.wait_ge(F.tanh_done, i + 1)
                flat = lambda v: v[:, :, :].rearrange("p t d -> p (t d)")
                dve.scalar_tensor_tensor(out=flat(F.u), in0=flat(F.th), scalar=1.0, in1=psum[F.name + "_v"][:, 0:S],
                                         op0=ALU.add, op1=ALU.mult).then_inc(F.gated, 1)
                dve.wait_ge(F.gated, i + 1)
                free(i)
                dve.scalar_tensor_tensor(out=flat(F.dst), in0=flat(F.u), scalar=0.5, in1=flat(F.src),
                                         op0=ALU.mult, op1=ALU.add).then_inc(F.x_ready, 1)

            def stats_f1(i):
                dve.wait_ge(x1_ready, i + 1)
                stats(norm_f1, x1, i)

            def stats_b(i):
                dve.wait_ge(f1.x_ready, i + 1)
                stats(norm_b, x2, i)

            def rest_b(i):
                dve.wait_ge(splitB, 3 * i + 1)
                dve.tensor_tensor(remB[:, :], qkS[:, :, :].rearrange("p n s -> p (n s)"), partsB[:, 0, :], ALU.subtract).then_inc(splitB_rem, 1)

            def last_b(i):
                dve.wait_ge(splitB_rem, i + 1)
                dve.wait_ge(splitB, 3 * i + 2)
                dve.tensor_tensor(partsB[:, 2, :], remB[:, :], partsB[:, 1, :], ALU.subtract).then_inc(splitB, 1)

            def keep_heads(i):
                dve.wait_ge(kv_psum, i + 1)
                dve.wait_ge(oB_psum, i)
                dve.tensor_tensor(state[:, :], psum["b_kv"][:, D:2 * D], same_head, ALU.mult).then_inc(state_ready, 1)

            def r_values():
                return psum["b_turn_o"][:, 0:S].rearrange("p (t d) -> p t d", t=T)

            def stats_r(i):
                dve.wait_ge(oBT_psum, i + 1)
                stats(norm_r, r_values(), i)

            def gated_b(i):
                dve.wait_ge(nT_ready, i + 1)
                dve.wait_ge(gate_ready, i + 1)
                dve.wait_ge(projB, i)
                dve.scalar_tensor_tensor(out=yT[:, :], in0=gate[:, :], scalar=1.0, in1=nT[:, :], op0=ALU.add, op1=ALU.mult).then_inc(yT_ready, 1)

            def residual_b(i):
                dve.wait_ge(projB, i + 1)
                dve.wait_ge(x2_copied, 16 * (i + 1))
                dve.tensor_tensor(x3[:, :, :].rearrange("p t d -> p (t d)"), x2_res[:, :, :].rearrange("p t d -> p (t d)"),
                                  psum["b_out"][:, S:2 * S], ALU.add).then_inc(projB_used, 1)

            def stats_f2(i):
                dve.wait_ge(projB_used, i + 1)
                stats(norm_f2, x3, i)

            def x2_free(i):
                dve.wait_ge(x2_copied, 16 * i)

            def x4_free(i):
                dve.wait_ge(out_done, 16 * i)

            def row_maxima(i, first, last):
                for k in range(first, last):
                    row_max(i, k)

            def slot(s):
                one, two, three, four, five = (running(s, n) for n in range(5))
                if three:
                    row_maxima(s - 2, 2, 5)
                if five:
                    stats_r(s - 4)
                if four:
                    ffn_out(f1, s - 3, x2_free)
                    stats_b(s - 3)
                if three:
                    row_maxima(s - 2, 5, 7)
                if four:
                    apply(norm_b, x2, zB, s - 3, zBT_psum)
                if three:
                    row_maxima(s - 2, 7, 9)
                if five:
                    apply(norm_r, r_values(), zR, s - 4, zRT_psum)
                if three:
                    row_maxima(s - 2, 9, 12)
                if five:
                    gated_b(s - 4)
                if two:
                    rope_products(s - 1)
                if five:
                    residual_b(s - 4)
                if four:
                    rest_b(s - 3)
                if five:
                    stats_f2(s - 4)
                if four:
                    last_b(s - 3)
                if five:
                    apply(norm_f2, x3, f2.z, s - 4)
                if two:
                    rest_a(s - 1)
                if one:
                    stats_a(s)
                if five:
                    ffn_mix(f2, s - 4)
                if two:
                    last_a(s - 1)
                if three:
                    normalise(s - 2)
                if one:
                    apply_a(s)
                if four:
                    keep_heads(s - 3)
                if three:
                    residual_a(s - 2)
                    stats_f1(s - 2)
                if five:
                    ffn_out(f2, s - 4, x4_free)
                if three:
                    apply(norm_f1, x1, f1.z, s - 2)
                if two:
                    row_maxima(s - 1, 0, 1)
                if three:
                    ffn_mix(f1, s - 2)
                if two:
                    row_maxima(s - 1, 1, 2)

            slots(dve, slot)

        @block.tensor
        def _(pe):
            def turn(dst, src, n=T):
                for t in range(n):
                    ins = pe.transpose(dst[:, t * P:(t + 1) * P], src[:, t, :], ident)
                return ins

            def add_bias(dst, first, width):
                return pe.matmul(dst, ones3[:, :], bias[:, first * D:first * D + width], start=False, stop=True, skip_group_check=True)

            read = {"a_turn": (zAT_ready, 1), "a_qk": (products, 2), "a_turn_qk": (splitA_rem, 1), "a_v": (vA_ready, 1),
                    "turn_max0": (maxT_ready, 2), "turn_max1": (maxT_ready, 2), "pv": (oA_ready, 1), "o_turn": (ctx_ready, 1),
                    "ctx_turn": (ctxT_ready, 1), "a_out": (x1_ready, 1),
                    "f1_turn": (f1.zT_ready, 1), "f1_rk": (f1.tanh_done, 1), "f1_v": (f1.gated, 1),
                    "b_turn": (zBT_ready, 1), "b_qk": (qkB_ready, 2), "b_vg": (gate_ready, 1), "turn_k": (kdec_ready, 1), "b_kv": (state_ready, 1),
                    "b_pv": (oB_ready, 1), "b_turn_o": (norm_r.done, 1), "b_turn_n": (nT_ready, 1), "b_out": (projB_used, 1),
                    "f2_turn": (f2.zT_ready, 1), "f2_rk": (f2.tanh_done, 1), "f2_v": (f2.gated, 1)}

            def bank_free(name, i):
                at = [n for n, _, _ in PSUM_USES].index(name)
                _, number, stage = PSUM_USES[at]
                for back in range(1, STAGES * len(PSUM_USES)):
                    prev, its, its_stage = PSUM_USES[(at - back) % len(PSUM_USES)]
                    if its != number:
                        continue
                    j = i + (stage - its_stage) + (at - back) // len(PSUM_USES)
                    if isinstance(j, int) and not 0 <= j < B:
                        continue
                    signal, count = read[prev]
                    return pe.wait_ge(signal, count * j + (1 if prev == "turn_max0" else count))

            pe.wait_ge(tables_in, 16 * 15)
            for n in range(3):
                ins = pe.transpose(bank[0][:, n * D:(n + 1) * D], wf[:, n, :], ident)
            ins.then_inc(wf_turned, 1)
            pe.wait_ge(bias_rows_in, 16 * PARTS)
            pe.wait_ge(cleared, 11)
            pe.wait_ge(masks_ready, 1)
            pe.wait_ge(wf_ready, 1)

            def a_turn(i):
                pe.wait_ge(norm_a.done, i + 1)
                bank_free("a_turn", i)
                turn(psum["a_turn"], zA).then_inc(zAT_psum, 1)

            def a_qk(i):
                pe.wait_ge(zAT_ready, i + 1)
                bank_free("a_qk", i)
                for t in range(T):
                    dst = psum["a_qk"][:, t * QKW:(t + 1) * QKW]
                    pe.matmul(dst, zAT[:, t * P:(t + 1) * P], wa[:, 0:2, :].rearrange("p n d -> p (n d)"), start=True, stop=False, skip_group_check=True)
                    ins = add_bias(dst, 0, QKW)
                ins.then_inc(qkA_psum, 1)

            def a_turn_qk(i):
                pe.wait_ge(rotated, i + 1)
                bank_free("a_turn_qk", i)
                for n in range(2):
                    for t in range(T):
                        ins = pe.transpose(psum["a_turn_qk"][:, n * S + t * P:n * S + (t + 1) * P], rot[:, t, n, :], ident)
                ins.then_inc(rotT_psum, 1)

            def a_v(i):
                pe.wait_ge(zAT_ready, i + 1)
                bank_free("a_v", i)
                for t in range(T):
                    dst = psum["a_v"][:, t * D:(t + 1) * D]
                    pe.matmul(dst, zAT[:, t * P:(t + 1) * P], wa[:, 2, :], start=True, stop=False, skip_group_check=True)
                    ins = add_bias(dst, 2, D)
                ins.then_inc(vA_psum, 1)

            def score_fill(i, k):
                if k % 6 == 0:
                    pe.wait_ge(stackA_in[k // 6], 16 * NSTACK * (i + 1))
                if k >= 2:
                    pe.wait_ge(scores_max, NFILL * i + k - 1)
                elif not (isinstance(i, int) and i <= 1):
                    pe.wait_ge(ret_copied, NRET * (i - 1))
                t, h0, heads = SCORE_FILLS[k]
                dst = ring[k % 2]
                if t == 0:
                    pe.matmul(dst[:, :], identb, future, start=True, stop=False, skip_group_check=True)
                else:
                    pe.matmul(dst[:, :].rearrange("p (h k) -> p h k", h=2)[:, :, P:S], identb,
                              future[:, 0:2 * P].rearrange("p (h k) -> p h k", h=2), start=True, stop=False, skip_group_check=True)
                w = (t + 1) * P
                for n in range(heads):
                    ins = pe.matmul(dst[:, n * w:(n + 1) * w], Qst[0:ROWS, h0 + n, t * P:(t + 1) * P], Kst[0:ROWS, h0 + n, 0:w],
                                    start=False, stop=True, skip_group_check=True)
                ins.then_inc(scores_full, 1)

            def scores(i, first, last):
                for k in range(first, last):
                    score_fill(i, k)

            def turn_max(i, half_):
                pe.wait_ge(maxp_ready, 2 * i + half_ + 1)
                bank_free(f"turn_max{half_}", i)
                apart(pe, "pe")
                dst = psum[f"turn_max{half_}"][0:PARTS * HALF, half_ * P:(half_ + 1) * P].bitcast(BF16)
                for t in range(T):
                    ins = pe.transpose(dst[:, t * P:(t + 1) * P], maxp[:, t, half_, :, :].rearrange("p n h -> p (n h)"), identb)
                ins.then_inc(maxT_psum, 1)

            def exp_fill(i, g):
                if g % 6 == 0:
                    pe.wait_ge(max_rows_in[g // 6], 16 * (i + 1))
                if g >= 2:
                    pe.wait_ge(exp_done, NFILL * i + g - 1)
                elif not (isinstance(i, int) and i == 0):
                    pe.wait_ge(exp_done, NFILL * i)
                _, kt, h0 = EXP_FILLS[g]
                dst = exp_ring[g % 2]
                w = S if kt == 0 else P
                for n in range(512 // w):
                    h = h0 + n
                    ins = pe.matmul(dst[:, n * w:(n + 1) * w], Kst[0:XROWS, h, kt * P:(kt + 1) * P], Qst[0:XROWS, h, S - w:S], start=True, stop=True, skip_group_check=True)
                ins.then_inc(st_full, 1)

            def exp_fills(i, first, last):
                for g in range(first, last):
                    exp_fill(i, g)

            def pv(i, half_, kt):
                pe.wait_ge(masked, NFILL * i + 6 * half_ + (4, 6)[kt])
                if half_ == 0 and kt == 0:
                    pe.wait_ge(vA_ready, i + 1)
                    bank_free("pv", i)
                o = half_ * S
                for n in range(2):
                    for j in range(NCT):
                        h = hs(half_, j, n)
                        rhs = P0[:, h, :] if kt == 0 else P1[:, h, :]
                        ins = pe.matmul(psum["pv"][j * CT:(j + 1) * CT, o + kt * P:o + S], VA[:, kt, h, :], rhs,
                                        start=(half_ == 0 and kt == 0 and n == 0), stop=(kt == 1 and n == 1), skip_group_check=True)
                if kt == 1:
                    ins.then_inc(pv_done, 1)

            def o_turn(i):
                pe.wait_ge(oA_ready, i + 1)
                bank_free("o_turn", i)
                for t in range(T):
                    for half_ in range(2):
                        ins = pe.transpose(psum["o_turn"][:, (2 * t + half_) * P:(2 * t + half_ + 1) * P], oA[:, half_ * S + t * P:half_ * S + (t + 1) * P], ident)
                ins.then_inc(oAT_psum, 1)

            def ctx_turn(i):
                pe.wait_ge(ctx_ready, i + 1)
                bank_free("ctx_turn", i)
                turn(psum["ctx_turn"], ctxA).then_inc(ctxT_psum, 1)

            def a_out(i):
                pe.wait_ge(ctxT_ready, i + 1)
                bank_free("a_out", i)
                for t in range(T):
                    dst = psum["a_out"][:, S + t * D:S + (t + 1) * D]
                    pe.matmul(dst, ctxT[:, t * P:(t + 1) * P], wa[:, 3, :], start=True, stop=False, skip_group_check=True)
                    ins = add_bias(dst, 3, D)
                ins.then_inc(projA, 1)

            def ffn_turn(F, i):
                pe.wait_ge(F.norm.done, i + 1)
                bank_free(F.name + "_turn", i)
                turn(psum[F.name + "_turn"], F.z).then_inc(F.turned, 1)

            def ffn_rk(F, i):
                pe.wait_ge(F.mixed, 2 * (i + 1))
                bank_free(F.name + "_rk", i)
                for t in range(T):
                    pe.matmul(psum[F.name + "_rk"][:, S + t * D:S + (t + 1) * D], F.mix[:, 0, t * P:(t + 1) * P], wfT[:, 0, :], start=True, stop=True)
                pe.matmul(psum[F.name + "_rk"][:, 0:S], wfT[:, 1, :], F.mix[:, 1, :], start=True, stop=True).then_inc(F.rk_ready, 1)

            def ffn_v(F, i):
                pe.wait_ge(F.squared, i + 1)
                bank_free(F.name + "_v", i)
                for t in range(T):
                    ins = pe.matmul(psum[F.name + "_v"][:, t * D:(t + 1) * D], F.ka[:, t * P:(t + 1) * P], wfT[:, 2, :], start=True, stop=True)
                ins.then_inc(F.v_ready, 1)

            def b_turn(i):
                pe.wait_ge(norm_b.done, i + 1)
                bank_free("b_turn", i)
                turn(psum["b_turn"], zB).then_inc(zBT_psum, 1)

            def b_qk(i):
                pe.wait_ge(zBT_ready, i + 1)
                bank_free("b_qk", i)
                for n in range(2):
                    ins = pe.matmul(psum["b_qk"][:, n * S:(n + 1) * S], wqk_dh[:, n, :], zBT[:, :], start=True, stop=True)
                ins.then_inc(qkB_psum, 1)

            def b_vg(i):
                pe.wait_ge(zBT_ready, i + 1)
                bank_free("b_vg", i)
                for t in range(T):
                    dst = psum["b_vg"][:, t * D:(t + 1) * D]
                    pe.matmul(dst, zBT[:, t * P:(t + 1) * P], wb[:, 2, :], start=True, stop=False, skip_group_check=True)
                    add_bias(dst, 4, D)
                pe.matmul(psum["b_vg"][:, S:2 * S], wb[:, 3, :], zBT[:, :], start=True, stop=True).then_inc(vg_psum, 1)

            def turn_k(i):
                bank_free("turn_k", i)
                pe.wait_ge(qkS_ready, i + 1)
                pe.transpose(psum["turn_k"][:, 0:D], qkS[:, 1, 0:P], ident).then_inc(kB_psum, 1)

            def b_kv(i):
                pe.wait_ge(kdec_ready, i + 1)
                pe.wait_ge(vB_ready, i + 1)
                bank_free("b_kv", i)
                first = quad_view(VB)[:, 0:NCT, :, :]
                pe.matmul(psum["b_kv"][:, D:2 * D], kdec[:, :], first, start=True, stop=True).then_inc(kv_psum, 1)

            def ret_fill(i, k):
                if k == 0:
                    pe.wait_ge(stackB_in, 16 * NSTACK * (i + 1))
                if k < 2:
                    pe.wait_ge(scores_max, NFILL * (min(i + 2, B) if isinstance(i, int) else i + 2))
                else:
                    pe.wait_ge(ret_copied, NRET * i + k - 1)
                t = k // 4
                for n in range(4):
                    h = 4 * (k % 4) + n
                    ins = pe.matmul(ring[k % 2][:, n * P:(n + 1) * P], Rk[:, h, t * P:(t + 1) * P], Rq[:, h, t * P:(t + 1) * P], start=True, stop=True, skip_group_check=True)
                ins.then_inc(ret_full, 1)

            def ret_fills(i, first, last):
                for k in range(first, last):
                    ret_fill(i, k)

            def b_pv(i, t):
                pe.wait_ge(ret_done, NRET * i + 4 * (t + 1))
                if t == 0:
                    bank_free("b_pv", i)
                if t == 1:
                    pe.wait_ge(state_ready, i + 1)
                    pe.matmul(psum["b_pv"][:, P:S], state[:, :], qkS[:, 0, P:S], start=False, stop=False, skip_group_check=True)
                for n in range(4):
                    for j in range(NCT):
                        h = 4 * j + n
                        ins = pe.matmul(psum["b_pv"][j * CT:(j + 1) * CT, t * P:(t + 1) * P], VB[:, t, h, :], PR[:, t, h, :],
                                        start=(t == 0 and n == 0), stop=(n == 3), skip_group_check=True)
                if t == 1:
                    ins.then_inc(oB_psum, 1)

            def b_turn_o(i):
                pe.wait_ge(oB_ready, i + 1)
                bank_free("b_turn_o", i)
                for t in range(T):
                    ins = pe.transpose(psum["b_turn_o"][:, t * P:(t + 1) * P], oB[:, t * P:(t + 1) * P], ident)
                ins.then_inc(oBT_psum, 1)

            def b_turn_n(i):
                pe.wait_ge(norm_r.done, i + 1)
                bank_free("b_turn_n", i)
                turn(psum["b_turn_n"], zR).then_inc(zRT_psum, 1)

            def b_out(i):
                pe.wait_ge(yT_ready, i + 1)
                bank_free("b_out", i)
                for t in range(T):
                    dst = psum["b_out"][:, S + t * D:S + (t + 1) * D]
                    pe.matmul(dst, yT[:, t * P:(t + 1) * P], wb[:, 4, :], start=True, stop=False, skip_group_check=True)
                    ins = add_bias(dst, 5, D)
                ins.then_inc(projB, 1)

            def slot(s):
                one, two, three, four, five = (running(s, n) for n in range(5))
                if three:
                    scores(s - 2, 3, 5)
                if five:
                    b_turn_o(s - 4)
                if three:
                    scores(s - 2, 5, 6)
                if four:
                    ffn_v(f1, s - 3)
                if two:
                    a_turn(s - 1)
                if three:
                    scores(s - 2, 6, 7)
                    a_v(s - 2)
                    scores(s - 2, 7, 9)
                if four:
                    b_turn(s - 3)
                if three:
                    turn_max(s - 2, 0)
                    scores(s - 2, 9, 10)
                if four:
                    b_qk(s - 3)
                if three:
                    scores(s - 2, 10, 11)
                if five:
                    b_turn_n(s - 4)
                if three:
                    scores(s - 2, 11, 12)
                if two:
                    a_qk(s - 1)
                if three:
                    exp_fills(s - 2, 0, 1)
                if five:
                    b_out(s - 4)
                if three:
                    exp_fills(s - 2, 1, 2)
                    turn_max(s - 2, 1)
                    exp_fills(s - 2, 2, 3)
                if four:
                    turn_k(s - 3)
                    b_vg(s - 3)
                if three:
                    exp_fills(s - 2, 3, 5)
                if two:
                    a_turn_qk(s - 1)
                if three:
                    exp_fills(s - 2, 5, 7)
                if five:
                    ffn_turn(f2, s - 4)
                if three:
                    exp_fills(s - 2, 7, 8)
                    pv(s - 2, 0, 0)
                    exp_fills(s - 2, 8, 10)
                    pv(s - 2, 0, 1)
                    exp_fills(s - 2, 10, 12)
                if five:
                    ffn_rk(f2, s - 4)
                if three:
                    pv(s - 2, 1, 0)
                    pv(s - 2, 1, 1)
                if four:
                    b_kv(s - 3)
                    ret_fills(s - 3, 0, 2)
                if three:
                    o_turn(s - 2)
                if four:
                    ret_fills(s - 3, 2, 4)
                if three:
                    ctx_turn(s - 2)
                if four:
                    ret_fills(s - 3, 4, 6)
                if three:
                    a_out(s - 2)
                if five:
                    ffn_v(f2, s - 4)
                if four:
                    ret_fills(s - 3, 6, 8)
                    b_pv(s - 3, 0)
                if two:
                    scores(s - 1, 0, 2)
                if three:
                    ffn_turn(f1, s - 2)
                if two:
                    scores(s - 1, 2, 3)
                if four:
                    b_pv(s - 3, 1)
                if three:
                    ffn_rk(f1, s - 2)

            slots(pe, slot)


_OUT = ((B, S, D), "float32")
_A = ["Wq", "bq", "Wk", "bk", "Wv", "bv", "Wo", "bo"]
_B = ["Wq", "bq", "Wk", "bk", "Wv", "bv", "Wg", "bg", "Wo", "bo", "gamma", "beta"]
_F = ["W_r", "W_k", "W_v", "mu_r", "mu_k"]


def kernel(**inputs):
    import concourse.bacc as _bacc
    from concourse.bass_utils import run_bass_kernel_spmd as _run

    nc = _bacc.Bacc("TRN2", target_bir_lowering=False, num_devices=1)
    arrays = {}

    def given(name, value):
        v = np.ascontiguousarray(value)
        arrays[f"in_{name}"] = v
        return nc.dram_tensor(f"in_{name}", v.shape, mybir.dt.from_np(v.dtype), kind="ExternalInput").ap()

    x = given("x", inputs["L0_attn_a_x"])
    a = {n: given(f"a_{n}", inputs[f"L0_attn_a_{n}"]) for n in _A}
    b = {n: given(f"b_{n}", inputs[f"L0_attn_b_{n}"]) for n in _B}
    f = {n: given(f"f_{n}", inputs[f"L0_ffn_{n}"]) for n in _F}
    c = {n: given(n, v) for n, v in constants().items()}
    out = nc.dram_tensor("out", _OUT[0], mybir.dt.from_np(np.dtype(_OUT[1])), kind="ExternalOutput").ap()
    build(nc, x, a, b, f, c, out)
    r = _run(nc, [arrays], core_ids=[0])
    return r.results[0]["out"]
```

```python
from contextlib import ExitStack

import concourse.bass as bass
from concourse import mybir
import numpy as np

ALU = mybir.AluOpType
ACT = mybir.ActivationFunctionType
AX_X = mybir.AxisListType.X
F32 = mybir.dt.float32
BF16 = mybir.dt.bfloat16

B, S, D = 8, 256, 128
P = 128
T = S // P
H, HD = 16, 8
PARTS = 3
PAIRS = PARTS * PARTS
KPARTS = 2 * PARTS - 1
HALF = H // 2
ROWS = HD * PAIRS
XROWS = ROWS + PARTS
SLOT = HD + 1
CT = 32
NCT = P // CT
SCALE = float(HD) ** -0.5
DECAY = 0.99
EPS = 1e-5
BIG = 1e30
QKW = 2 * D
STAGES = 5
PSUM_USES = [
    ("f1_v", 3, 3), ("turn_max1", 0, 2), ("pv", 3, 2), ("b_turn_o", 1, 4), ("b_turn", 0, 3), ("b_qk", 2, 3), ("b_turn_n", 1, 4),
    ("a_turn", 1, 0), ("b_out", 0, 4), ("turn_k", 2, 3), ("a_v", 0, 1), ("o_turn", 3, 2), ("b_vg", 1, 3), ("a_qk", 0, 0),
    ("ctx_turn", 3, 2), ("f2_turn", 2, 4), ("b_kv", 1, 3), ("a_out", 2, 2), ("turn_max0", 3, 1), ("f2_rk", 0, 4), ("ret0", 3, 3),
    ("ret1", 0, 3), ("ret2", 1, 3), ("f1_turn", 3, 2), ("ret3", 2, 3), ("a_turn_qk", 0, 0), ("ret4", 3, 3), ("ret5", 1, 3),
    ("ret6", 2, 3), ("f1_rk", 3, 2), ("ret7", 0, 3), ("f2_v", 1, 4), ("b_pv", 2, 3),
]


def constants():
    freq = np.power(np.float32(10000.0), np.float32(-2.0) * np.arange(D // 2, dtype=np.float32) / np.float32(D))
    ang = (np.arange(S, dtype=np.float32)[:, None] * freq.astype(np.float32)[None, :]).astype(np.float32)
    cos, sin = np.cos(ang), np.sin(ang)

    def rope(first, second):
        t = np.concatenate([first, second], axis=1).reshape(T, P, 1, D)
        return np.repeat(t, 2, axis=2).transpose(1, 0, 2, 3).reshape(P, T * 2 * D).astype(np.float32)

    i = np.arange(P)
    same_head = (i[:, None] % H == i[None, :] // HD).astype(np.float32)
    from_middle = np.power(np.float64(DECAY), np.arange(S) - S // 2)
    qk_decay = np.tile(np.concatenate([from_middle * SCALE, 1.0 / from_middle])[None, :], (P, 1)).astype(np.float32)
    future = np.where(i[None, :] > i[:, None], -BIG, 0.0)
    return {
        "c_rope": np.concatenate([rope(cos, sin), rope(sin, cos)], axis=1),
        "c_f32": np.concatenate([np.eye(P, dtype=np.float32), same_head, qk_decay], axis=1),
        "c_masks": np.concatenate([np.eye(P), np.tile(future, (1, 4))], axis=1).astype(np.float32),
    }


def build(nc, x, a, b, f, c, out):
    ctx = ExitStack()
    with ctx:
        def sb(name, shape, dt=F32):
            return ctx.enter_context(nc.sbuf_tensor(name, shape, dt))

        def sem(name):
            return ctx.enter_context(nc.semaphore(name))

        rope = sb("rope", [P, 2, T * QKW])
        cf = sb("cf", [P, 2 * P + 2 * S])
        cb = sb("cb", [P, P + 4 * P], BF16)
        ident, same_head, qk_decay = cf[:, 0:P], cf[:, P:2 * P], cf[:, 2 * P:]
        identb, future = cb[:, 0:P], cb[:, P:5 * P]
        wa = sb("wa", [P, 4, D])
        wb = sb("wb", [P, 5, D])
        wqk_dh = sb("wqk_dh", [P, 2, D])
        wf = sb("wf", [P, 3, D])
        wfT = sb("wfT", [P, 3, D])
        vecs = sb("vecs", [P, 7])
        half = sb("half", [P, 3])
        NB = 6
        brow = sb("brow", [1, 3, NB * D])
        browp = sb("browp", [1, PARTS, NB * D], BF16)
        bias = sb("bias", [PARTS, NB * D], BF16)
        minus_half = sb("minus_half", [P, T])
        ones1 = sb("ones1", [1, P])
        ones3 = sb("ones3", [PARTS, P], BF16)

        x_in = sb("x_in", [P, T, D])
        zA = sb("zA", [P, T, D])
        zAT = sb("zAT", [P, S])
        masks_f32 = sb("masks_f32", [P, 5 * P])
        prod = sb("prod", [P, 2, T * QKW])
        rot = sb("rot", [P, T, 2, D])
        partsA = sb("partsA", [P, PARTS, 2 * S], BF16)
        remA = sb("remA", [P, 2 * S])
        Qst = sb("Qst", [XROWS, H, S], BF16)
        Kst = sb("Kst", [XROWS, H, S], BF16)
        mx = sb("mx", [P, T, H])
        mrem = sb("mrem", [P, T, H])
        maxp = sb("maxp", [P, T, 2, PARTS, HALF], BF16)
        maxT = sb("maxT", [PARTS * HALF, 2, S], BF16)
        VA = sb("VA", [P, T, H, CT])
        x_res = sb("x_res", [P, T, D])
        P0 = sb("P0", [P, H, S])
        P1 = sb("P1", [P, H, P])
        oA = sb("oA", [P, 2 * S])
        rsum = sb("rsum", [P, T * H // 2, 2])
        ctxA = sb("ctxA", [P, T, D])
        ctxT = sb("ctxT", [P, S])
        x1 = sb("x1", [P, T, D])
        x2 = sb("x2", [P, T, D])
        zB = sb("zB", [P, T, D])
        zBT = sb("zBT", [P, S])
        qkS = sb("qkS", [P, 2, S])
        partsB = sb("partsB", [P, PARTS, 2 * S], BF16)
        remB = sb("remB", [P, 2 * S])
        Rq = sb("Rq", [ROWS, H, S], BF16)
        Rk = sb("Rk", [ROWS, H, S], BF16)
        VB = sb("VB", [P, T, H, CT])
        gate = sb("gate", [P, S])
        kdec = sb("kdec", [P, D])
        state = sb("state", [P, D])
        x2_res = sb("x2_res", [P, T, D])
        PR = sb("PR", [P, T, H, P])
        oB = sb("oB", [P, S])
        zR = sb("zR", [P, T, D])
        nT = sb("nT", [P, S])
        yT = sb("yT", [P, S])
        x3 = sb("x3", [P, T, D])
        x4 = sb("x4", [P, T, D])

        bank = [ctx.enter_context(nc.psum_tensor(f"bank{n}", [P, 512], F32)) for n in range(8)]
        ring = bank[0:2]
        exp_ring = bank[2:4]
        psum = {name: bank[4 + n] for name, n, _ in PSUM_USES}

        class Norm:
            def __init__(self, name):
                self.st = sb(f"{name}_st", [P, T, 6])
                self.mv = sb(f"{name}_mv", [P, T, 2])
                self.var = sb(f"{name}_var", [P, T])
                self.rstd = sb(f"{name}_rstd", [P, T])
                self.stats, self.moments, self.shifted, self.rdev, self.done = (
                    sem(f"{name}_{n}") for n in ("stats", "moments", "shifted", "rdev", "done"))

        norm_a, norm_f1, norm_b, norm_r, norm_f2 = (Norm(n) for n in ("norm_a", "norm_f1", "norm_b", "norm_r", "norm_f2"))

        class Ffn:
            def __init__(self, name, norm, src, dst):
                self.name, self.norm, self.src, self.dst = name, norm, src, dst
                self.z = sb(f"{name}_z", [P, T, D])
                self.zT = sb(f"{name}_zT", [P, 1 + S])
                self.dz = sb(f"{name}_dz", [P, S])
                self.mix = sb(f"{name}_mix", [P, 2, S])
                self.kr = sb(f"{name}_kr", [P, S])
                self.ka = sb(f"{name}_ka", [P, S])
                self.th = sb(f"{name}_th", [P, T, D])
                self.u = sb(f"{name}_u", [P, T, D])
                self.turned = sem(f"{name}_turned")
                self.zT_ready = sem(f"{name}_zT_ready")
                self.dz_ready = sem(f"{name}_dz_ready")
                self.mixed = sem(f"{name}_mixed")
                self.rk_ready = sem(f"{name}_rk_ready")
                self.relu_done = sem(f"{name}_relu_done")
                self.tanh_done = sem(f"{name}_tanh_done")
                self.squared = sem(f"{name}_squared")
                self.v_ready = sem(f"{name}_v_ready")
                self.gated = sem(f"{name}_gated")
                self.x_ready = sem(f"{name}_x_ready")

        f1 = Ffn("f1", norm_f1, x1, x2)
        f2 = Ffn("f2", norm_f2, x3, x4)

        ident_in, biases_in, qk_in, rope_in, masks_in, bias_rows_in, wf_in, vecs_in, late_in = (
            sem(n) for n in ("ident_in", "biases_in", "qk_in", "rope_in", "masks_in", "bias_rows_in", "wf_in", "vecs_in", "late_in"))
        first_cleared = sem("first_cleared")
        masks_ready, ordered = sem("masks_ready"), sem("ordered")
        bias_split, cleared, wf_turned, wf_ready, halved = (sem(n) for n in ("bias_split", "cleared", "wf_turned", "wf_ready", "halved"))
        xin_in, zAT_psum, zAT_ready, qkA_psum, products, rotated = (
            sem(n) for n in ("xin_in", "zAT_psum", "zAT_ready", "qkA_psum", "products", "rotated"))
        rotT_psum, splitA, splitA_rem, vA_psum, vA_ready = (
            sem(n) for n in ("rotT_psum", "splitA", "splitA_rem", "vA_psum", "vA_ready"))
        stackA_in, stackB_in, max_rows_in = ([sem(f"{n}_{half_}") for half_ in range(2)] for n in ("stackA_in", "stackB_in", "max_rows_in"))
        scores_full, scores_max, maxp_step, maxp_ready, maxT_psum, maxT_ready = (
            sem(n) for n in ("scores_full", "scores_max", "maxp_step", "maxp_ready", "maxT_psum", "maxT_ready"))
        st_full, exp_done, masked, pv_done, oA_ready, oAT_psum, rsum_ready, ctx_ready, ctxT_psum, ctxT_ready, projA, x1_ready = (
            sem(n) for n in ("st_full", "exp_done", "masked", "pv_done", "oA_ready", "oAT_psum", "rsum_ready", "ctx_ready",
                             "ctxT_psum", "ctxT_ready", "projA", "x1_ready"))
        xres_in, zBT_psum, zBT_ready, qkB_psum, splitB, splitB_rem = (
            sem(n) for n in ("xres_in", "zBT_psum", "zBT_ready", "qkB_psum", "splitB", "splitB_rem"))
        vg_psum, vB_ready, gate_ready, kB_psum, kdec_ready, qkS_ready, kv_psum, state_ready, x2_copied = (
            sem(n) for n in ("vg_psum", "vB_ready", "gate_ready", "kB_psum", "kdec_ready", "qkS_ready", "kv_psum", "state_ready", "x2_copied"))
        ret_full, ret_copied, ret_done, oB_psum, oB_ready, oBT_psum, zRT_psum, nT_ready, yT_ready, projB, out_done = (
            sem(n) for n in ("ret_full", "ret_copied", "ret_done", "oB_psum", "oB_ready", "oBT_psum", "zRT_psum", "nT_ready", "yT_ready", "projB", "out_done"))

        NFILL = T * H * P * T // 512 - H * P // 512
        NRET = T * H * P // 512
        NMASK = 4
        NSTACK = 2
        NSPILL = 3

        def running(s, stage):
            return not isinstance(s, int) or 0 <= s - stage < B

        passed = {e: sem(f"passed_{e}") for e in ("pe", "dve", "pool", "sp")}

        def apart(eng, name):
            eng.sem_inc(passed[name], 1)

        def slots(eng, body):
            for s in range(STAGES):
                body(s)
            with eng.Fori(STAGES, B) as s:
                body(s)
            for s in range(B, B + STAGES - 1):
                body(s)

        def hs(set_, j, n):
            return set_ * 8 + 2 * j + n

        RET_FILLS = [(t, h) for half_ in range(2) for t in range(T) for h in range(8 * half_, 8 * half_ + 8, 4)]
        SCORE_FILLS = [(t, h, n) for half_ in range(2) for t, n in ((0, 4), (1, 2)) for h in range(8 * half_, 8 * half_ + 8, n)]
        EXP_FILLS = [(half_, kt, h) for half_ in range(2) for kt, n in ((0, 2), (1, 4)) for h in range(8 * half_, 8 * half_ + 8, n)]

        scratchA, scratchB = ([nc.dram_tensor(f"parts_{w}_{n}", (parts, D, S), BF16, kind="Internal").ap()
                               for n, parts in (("q", PARTS), ("k", KPARTS))] for w in "ab")
        spilledA, spilledB, projB_used = sem("spilledA"), sem("spilledB"), sem("projB_used")

        block = ctx.enter_context(nc.Block())

        def pair_view(v):
            whole = v[:, :, :, :]
            return bass.AP(whole.tensor, whole.offset, [whole.ap[0], [2 * CT, T * H // 2], [CT + SLOT, 2], [1, HD]])

        def quad_view(v):
            whole = v[:, :, :, :]
            return bass.AP(whole.tensor, whole.offset, [whole.ap[0], [4 * CT, T * H // 4], [CT + HD, 4], [1, HD]])

        @block.sync
        def _(sp):
            sp.dma_start(x_in[:, :, :], x[0].rearrange("(t p) d -> p t d", p=P)).then_inc(xin_in, 16)
            sp.dma_start(cf[:, :], c["c_f32"]).then_inc(ident_in, 16)
            rows = [a["bq"], a["bk"], a["bv"], a["bo"], b["bv"], b["bo"]]
            for n in range(2):
                sp.dma_start(wa[:, n, :], (a["Wq"], a["Wk"])[n]).then_inc(qk_in, 16)
                sp.dma_start(brow[0:1, 0, n * D:(n + 1) * D], rows[n].rearrange("(o n) -> o n", o=1)).then_inc(qk_in, 16)
            sp.dma_start(rope[:, :, :], c["c_rope"].rearrange("p (a n) -> p a n", a=2)).then_inc(rope_in, 16)
            for n in range(2, NB):
                sp.dma_start(brow[0:1, 0, n * D:(n + 1) * D], rows[n].rearrange("(o n) -> o n", o=1)).then_inc(biases_in, 16)
            sp.dma_start(masks_f32[:, :], c["c_masks"]).then_inc(masks_in, 16)
            for n, w in ((2, a["Wv"]), (3, a["Wo"])):
                sp.dma_start(wa[:, n, :], w).then_inc(late_in, 16)
            for n, w in enumerate((f["W_r"], f["W_k"], f["W_v"])):
                sp.dma_start(wf[:, n, :], w).then_inc(wf_in, 16)
            with nc.allow_non_contiguous_dma(reason="seven vectors onto partitions, once"):
                for n, w in enumerate((f["mu_r"], f["mu_k"], b["bg"], b["gamma"], b["beta"])):
                    sp.dma_start(vecs[:, n:n + 1], w.rearrange("(n o) -> n o", o=1)).then_inc(vecs_in, 16)
                for n, w in enumerate((b["bq"], b["bk"])):
                    sp.dma_start(vecs[:, 5 + n:6 + n], bass.AP(w.tensor, w.offset, [[1, HD], [HD, H], [1, 1]])).then_inc(vecs_in, 16)
            for n, w in enumerate((b["Wq"], b["Wk"], b["Wv"], b["Wg"], b["Wo"])):
                sp.dma_start(wb[:, n, :], w).then_inc(late_in, 16)
            sp.wait_ge(bias_split, 5)
            for n in range(PARTS):
                sp.dma_start(bias[n:n + 1, :], browp[0:1, n, :]).then_inc(bias_rows_in, 16)

            def load_x(i):
                if isinstance(i, int) and i == 0:
                    return
                sp.wait_ge(norm_a.done, i)
                sp.dma_start(x_in[:, :, :], x[i].rearrange("(t p) d -> p t d", p=P)).then_inc(xin_in, 16)

            def load_x_res(i):
                sp.wait_ge(x1_ready, i)
                sp.dma_start(x_res[:, :, :], x[i].rearrange("(t p) d -> p t d", p=P)).then_inc(xres_in, 16)

            def spill_k_again(parts, k_scratch, spilled):
                sp.dma_start(k_scratch[PARTS:KPARTS].rearrange("m r t -> r m t"), parts[:, 0:PARTS - 1, S:2 * S]).then_inc(spilled, 16)

            def spill(parts, scratch, spilled):
                for n in range(2):
                    sp.dma_start(scratch[n][0:PARTS].rearrange("m r t -> r m t"), parts[:, :, n * S:(n + 1) * S]).then_inc(spilled, 16)

            def stacks(q_st, k_st, scratch, heads, landed):
                rows, run = PARTS * HD, (heads.stop - heads.start) * S
                for st, part, step in ((k_st, scratch[1], D * S), (q_st, scratch[0], 0)):
                    src = bass.AP(part.tensor, part.offset + heads.start * S, [[step, PARTS], [H * S, rows], [1, run]])
                    sp.dma_start(st[0:ROWS, heads, :], src).then_inc(landed, 16)

            def max_rows(i, half_):
                sp.wait_ge(maxT_ready, 2 * i + half_ + 1)
                sp.dma_start(Qst[ROWS:XROWS, half_ * HALF:(half_ + 1) * HALF, :],
                             maxT[:, half_, :]).then_inc(max_rows_in[half_], 16)

            def copy_x2(i):
                sp.wait_ge(projB_used, i)
                apart(sp, "sp")
                sp.wait_ge(f1.x_ready, i + 1)
                sp.dma_start(x2_res[:, :, :], x2[:, :, :]).then_inc(x2_copied, 16)

            def spill_b_early(i):
                sp.wait_ge(splitB, 3 * i + 2)
                spill_k_again(partsB, scratchB[1], spilledB)

            def spill_b(i):
                sp.wait_ge(splitB, 3 * i + 3)
                spill(partsB, scratchB, spilledB)

            def stack_b(i, half_):
                if not (isinstance(i, int) and i == 0):
                    sp.wait_ge(ret_full, NRET * (i - 1) + 4 * (half_ + 1))
                    apart(sp, "sp")
                sp.wait_ge(spilledB, 16 * NSPILL * (i + 1))
                stacks(Rq, Rk, scratchB, slice(half_ * HALF, (half_ + 1) * HALF), stackB_in[half_])

            def spill_a_early(i):
                sp.wait_ge(splitA, 3 * i + 2)
                spill_k_again(partsA, scratchA[1], spilledA)

            def spill_a(i):
                sp.wait_ge(splitA, 3 * i + 3)
                spill(partsA, scratchA, spilledA)

            def stack_a(i, half_):
                if not (isinstance(i, int) and i == 0):
                    sp.wait_ge(st_full, NFILL * (i - 1) + 6 * (half_ + 1))
                    apart(sp, "sp")
                sp.wait_ge(spilledA, 16 * NSPILL * (i + 1))
                stacks(Qst, Kst, scratchA, slice(half_ * HALF, (half_ + 1) * HALF), stackA_in[half_])

            def store(i):
                sp.wait_ge(f2.x_ready, i + 1)
                sp.dma_start(out[i].rearrange("(t p) d -> p t d", p=P), x4[:, :, :]).then_inc(out_done, 16)

            def slot(s):
                one, two, three, four, five = (running(s, n) for n in range(5))
                if three:
                    max_rows(s - 2, 1)
                if one:
                    load_x(s)
                if two:
                    stack_a(s - 1, 0)
                    stack_a(s - 1, 1)
                if four:
                    spill_b_early(s - 3)
                    spill_b(s - 3)
                    copy_x2(s - 3)
                    stack_b(s - 3, 0)
                    stack_b(s - 3, 1)
                if two:
                    max_rows(s - 1, 0)
                if one:
                    spill_a_early(s)
                    spill_a(s)
                if five:
                    store(s - 4)
                if two:
                    load_x_res(s - 1)

            slots(sp, slot)
            sp.wait_ge(out_done, 16 * B)

        @block.gpsimd
        def _(pool):
            pool.memset(minus_half[:, :], -0.5).then_inc(first_cleared, 1)
            pool.memset(ones1[:, :], 1.0).then_inc(first_cleared, 1)
            pool.memset(f1.zT[:, 0:1], 0.0).then_inc(first_cleared, 1)
            pool.memset(f2.zT[:, 0:1], 0.0).then_inc(first_cleared, 1)
            pool.wait_ge(first_cleared, 4)

            def clear():
                pool.memset(ones3[:, :], 1.0).then_inc(cleared, 1)
                pool.memset(VA[:, :, :, :], 0.0).then_inc(cleared, 1)
                pool.memset(VB[:, :, :, :], 0.0).then_inc(cleared, 1)
                pool.wait_ge(cleared, 3)
                pool.memset(Kst[64:XROWS, :, :], -1.0).then_inc(cleared, 1)
                pool.wait_ge(cleared, 4)
                va = VA[:, :, :, :].rearrange("p t (g n) c -> p (t g) n c", n=2)
                for n in range(2):
                    pool.memset(va[:, :, n, n * SLOT + HD:n * SLOT + HD + 1], 1.0).then_inc(cleared, 1)

            def order_weights():
                pool.wait_ge(late_in, 16 * 7)
                for n in range(2):
                    pool.tensor_copy(wqk_dh[:, n, :].rearrange("c (d h) -> c h d", h=H), wb[:, n, :].rearrange("c (h d) -> c h d", d=HD)).then_inc(ordered, 1)

            def deviation(N, i):
                pool.wait_ge(N.moments, i + 1)
                apart(pool, "pool")
                pool.tensor_scalar(N.var[:, :], N.mv[:, :, 1], EPS, None, ALU.add).then_inc(N.shifted, 1)
                pool.wait_ge(N.shifted, i + 1)
                pool.wait_ge(N.done, i)
                pool.tensor_tensor(N.rstd[:, :], N.var[:, :], minus_half[:, :], ALU.pow).then_inc(N.rdev, 1)
                if N is norm_a and isinstance(i, int) and i == 0:
                    clear()

            def rotate(i):
                pool.wait_ge(products, 2 * (i + 1))
                pool.wait_ge(rotT_psum, i)
                turned = rot[:, :, :, :].rearrange("p t w (d h) -> p (t w) h d", h=H)
                first, second = (prod[:, n, :].rearrange("p (w h d) -> p w h d", w=2 * T, d=HD) for n in range(2))
                pool.tensor_tensor(turned, first, second, ALU.subtract).then_inc(rotated, 1)
                if isinstance(i, int) and i == 0:
                    order_weights()

            def split_max(i, half_):
                step, heads = 6 * i + 3 * half_, slice(half_ * HALF, (half_ + 1) * HALF)
                pool.wait_ge(scores_max, NFILL * i + 6 * (half_ + 1))
                pool.wait_ge(maxT_psum, 2 * i)
                apart(pool, "pool")
                pool.tensor_copy(maxp[:, :, half_, 0, :], mx[:, :, heads]).then_inc(maxp_step, 1)
                pool.wait_ge(maxp_step, step + 1)
                pool.tensor_tensor(mrem[:, :, heads], mx[:, :, heads], maxp[:, :, half_, 0, :], ALU.subtract).then_inc(maxp_step, 1)
                pool.wait_ge(maxp_step, step + 2)
                apart(pool, "pool")
                pool.tensor_copy(maxp[:, :, half_, 1, :], mrem[:, :, heads]).then_inc(maxp_step, 1)
                pool.wait_ge(maxp_step, step + 3)
                pool.tensor_tensor(maxp[:, :, half_, 2, :], mrem[:, :, heads], maxp[:, :, half_, 1, :], ALU.subtract).then_inc(maxp_ready, 1)

            def mask(i, m):
                half_, m = divmod(m, NMASK)
                g = 6 * half_ + (0, 2, 4, 5)[m]
                last = 6 * half_ + (1, 3, 4, 5)[m]
                _, kt, h = EXP_FILLS[g]
                pool.wait_ge(exp_done, NFILL * i + last + 1)
                apart(pool, "pool")
                blockp = P0[:, h:h + 4, 0:P] if kt == 0 else P1[:, h:h + 4, :]
                pool.affine_select(out=blockp, in_=blockp, compare_op=ALU.is_ge, fill=0.0, base=0,
                                   pattern=[[0, 4], [1, P]], channel_multiplier=-1).then_inc(masked, 1)

            def square(F, i):
                pool.wait_ge(F.relu_done, i + 1)
                pool.tensor_tensor(F.ka[:, :], F.kr[:, :], F.kr[:, :], ALU.mult).then_inc(F.squared, 1)

            def ret_mask(i, k):
                pool.wait_ge(ret_copied, NRET * i + k + 1)
                apart(pool, "pool")
                t, h = RET_FILLS[k]
                pool.affine_select(out=PR[:, t, h:h + 4, :], in_=PR[:, t, h:h + 4, :], compare_op=ALU.is_ge, fill=0.0, base=0,
                                   pattern=[[0, 4], [1, P]], channel_multiplier=-1).then_inc(ret_done, 1)

            def ret_masks(i, first, last):
                for k in range(first, last):
                    ret_mask(i, k)

            def masks(i, first, last):
                for g in range(first, last):
                    mask(i, g)

            def slot(s):
                one, two, three, four, five = (running(s, n) for n in range(5))
                if three:
                    split_max(s - 2, 1)
                if five:
                    ret_masks(s - 4, 7, 8)
                if three:
                    masks(s - 2, 0, 2)
                if four:
                    deviation(norm_b, s - 3)
                if three:
                    masks(s - 2, 2, 4)
                if five:
                    deviation(norm_r, s - 4)
                if one:
                    deviation(norm_a, s)
                if three:
                    masks(s - 2, 4, 8)
                if five:
                    deviation(norm_f2, s - 4)
                if two:
                    split_max(s - 1, 0)
                if one:
                    rotate(s)
                if three:
                    deviation(norm_f1, s - 2)
                if five:
                    square(f2, s - 4)
                if four:
                    ret_masks(s - 3, 0, 7)
                if three:
                    square(f1, s - 2)

            slots(pool, slot)

        @block.scalar
        def _(act):
            def prepare():
                act.wait_ge(wf_turned, 1)
                act.activation(wfT[:, :, :].rearrange("p a n -> p (a n)"), ring[0][:, 0:3 * D], ACT.Copy).then_inc(wf_ready, 1)

            def norm_turn(i):
                act.wait_ge(zAT_psum, i + 1)
                act.wait_ge(vA_psum, i)
                act.activation(zAT[:, :], psum["a_turn"][:, 0:S], ACT.Copy).then_inc(zAT_ready, 1)
                if isinstance(i, int) and i == 0:
                    prepare()

            def split_a(i):
                act.wait_ge(rotT_psum, i + 1)
                for half_ in range(2):
                    act.wait_ge(stackA_in[half_], 16 * NSTACK * i)
                act.activation(partsA[:, 0, :], psum["a_turn_qk"][:, :], ACT.Copy).then_inc(splitA, 1)

            def split_a_2(i):
                act.wait_ge(splitA_rem, i + 1)
                act.activation(partsA[:, 1, :], remA[:, :], ACT.Copy).then_inc(splitA, 1)

            def v_a(i):
                if isinstance(i, int) and i == 0:
                    act.wait_ge(cleared, 6)
                act.wait_ge(vA_psum, i + 1)
                act.wait_ge(pv_done, 2 * i)
                act.activation(pair_view(VA), psum["a_v"][:, 0:T * D].rearrange("p (g n d) -> p g n d", n=2, d=HD), ACT.Copy).then_inc(vA_ready, 1)

            def max_turn(i, half_):
                act.wait_ge(maxT_psum, 2 * i + half_ + 1)
                act.wait_ge(max_rows_in[half_], 16 * i)
                act.activation(maxT[:, half_, :], psum[f"turn_max{half_}"][0:PARTS * HALF, half_ * P:(half_ + 1) * P].bitcast(BF16), ACT.Copy).then_inc(maxT_ready, 1)

            def exponential(i, g):
                _, kt, h = EXP_FILLS[g]
                act.wait_ge(st_full, NFILL * i + g + 1)
                if g == 0:
                    act.wait_ge(pv_done, 2 * i)
                dst = P0[:, h:h + 2, :] if kt == 0 else P1[:, h:h + 4, :]
                act.activation(dst.rearrange("p h q -> p (h q)"), exp_ring[g % 2][:, :], ACT.Exp, scale=SCALE).then_inc(exp_done, 1)

            def o_a(i):
                act.wait_ge(pv_done, 2 * (i + 1))
                act.wait_ge(oAT_psum, i)
                act.activation(oA[:, :], psum["pv"][:, :], ACT.Copy).then_inc(oA_ready, 1)

            def ctx_turn(i):
                act.wait_ge(ctxT_psum, i + 1)
                act.wait_ge(projA, i)
                act.activation(ctxT[:, :], psum["ctx_turn"][:, 0:S], ACT.Copy).then_inc(ctxT_ready, 1)

            def ffn_zT(F, i):
                act.wait_ge(F.turned, i + 1)
                act.activation(F.zT[:, 1:1 + S], psum[F.name + "_turn"][:, 0:S], ACT.Copy).then_inc(F.zT_ready, 1)

            def ffn_act(F, i):
                act.wait_ge(F.rk_ready, i + 1)
                act.activation(F.kr[:, :], psum[F.name + "_rk"][:, 0:S], ACT.Relu).then_inc(F.relu_done, 1)
                act.activation(F.th[:, :, :].rearrange("p t d -> p (t d)"), psum[F.name + "_rk"][:, S:2 * S], ACT.Tanh, scale=0.5).then_inc(F.tanh_done, 1)

            def b_turn(i):
                act.wait_ge(zBT_psum, i + 1)
                act.wait_ge(vg_psum, i)
                act.activation(zBT[:, :], psum["b_turn"][:, 0:S], ACT.Copy).then_inc(zBT_ready, 1)

            def split_b(i):
                act.wait_ge(qkS_ready, i + 1)
                for half_ in range(2):
                    act.wait_ge(stackB_in[half_], 16 * NSTACK * i)
                act.activation(partsB[:, 0, :], qkS[:, :, :].rearrange("p n s -> p (n s)"), ACT.Copy).then_inc(splitB, 1)

            def split_b_2(i):
                act.wait_ge(splitB_rem, i + 1)
                act.activation(partsB[:, 1, :], remB[:, :], ACT.Copy).then_inc(splitB, 1)

            def b_vg(i):
                if isinstance(i, int) and i == 0:
                    act.wait_ge(vecs_in, 16 * 7)
                    act.wait_ge(cleared, 6)
                    act.mul(half[:, :], vecs[:, 2:5], 0.5).then_inc(halved, 1)
                    act.wait_ge(halved, 1)
                act.wait_ge(vg_psum, i + 1)
                act.wait_ge(oB_psum, i)
                act.activation(quad_view(VB), psum["b_vg"][:, 0:T * D].rearrange("p (g n d) -> p g n d", n=4, d=HD), ACT.Copy).then_inc(vB_ready, 1)
                act.wait_ge(yT_ready, i)
                act.activation(gate[:, :], psum["b_vg"][:, S:2 * S], ACT.Tanh, bias=half[:, 0:1], scale=0.5).then_inc(gate_ready, 1)

            def b_k(i):
                act.wait_ge(kB_psum, i + 1)
                act.activation(kdec[:, :], psum["turn_k"][:, 0:D], ACT.Copy).then_inc(kdec_ready, 1)

            def o_b(i):
                act.wait_ge(oB_psum, i + 1)
                act.wait_ge(oBT_psum, i)
                act.activation(oB[:, :], psum["b_pv"][:, 0:S], ACT.Copy).then_inc(oB_ready, 1)

            def affine_b(i):
                act.wait_ge(zRT_psum, i + 1)
                act.wait_ge(yT_ready, i)
                act.activation(nT[:, :], psum["b_turn_n"][:, 0:S], ACT.Identity, bias=half[:, 2:3], scale=half[:, 1:2]).then_inc(nT_ready, 1)

            def ret_copy(i, k):
                act.wait_ge(ret_full, NRET * i + k + 1)
                if k == 0:
                    act.wait_ge(oB_psum, i)
                t, h = RET_FILLS[k]
                act.activation(PR[:, t, h:h + 4, :].rearrange("p h q -> p (h q)"), psum[f"ret{k}"][:, :], ACT.Copy).then_inc(ret_copied, 1)

            def exps(i, first, last):
                for g in range(first, last):
                    exponential(i, g)

            def ret_copies(i, first, last):
                for k in range(first, last):
                    ret_copy(i, k)

            def slot(s):
                one, two, three, four, five = (running(s, n) for n in range(5))
                if five:
                    ret_copies(s - 4, 5, 7)
                if two:
                    split_a_2(s - 1)
                if four:
                    ffn_act(f1, s - 3)
                if three:
                    exps(s - 2, 0, 2)
                if five:
                    ret_copies(s - 4, 7, 8)
                if three:
                    exps(s - 2, 2, 4)
                    max_turn(s - 2, 1)
                    exps(s - 2, 4, 5)
                if five:
                    o_b(s - 4)
                if three:
                    exps(s - 2, 5, 7)
                if four:
                    b_turn(s - 3)
                if three:
                    exps(s - 2, 7, 10)
                if five:
                    affine_b(s - 4)
                if four:
                    split_b(s - 3)
                if three:
                    exps(s - 2, 10, 12)
                if four:
                    split_b_2(s - 3)
                if three:
                    o_a(s - 2)
                if one:
                    norm_turn(s)
                if four:
                    b_k(s - 3)
                if two:
                    v_a(s - 1)
                if four:
                    b_vg(s - 3)
                if five:
                    ffn_zT(f2, s - 4)
                if three:
                    ctx_turn(s - 2)
                if two:
                    max_turn(s - 1, 0)
                if five:
                    ffn_act(f2, s - 4)
                if four:
                    ret_copies(s - 3, 0, 3)
                if three:
                    ffn_zT(f1, s - 2)
                if four:
                    ret_copies(s - 3, 3, 4)
                if one:
                    split_a(s)
                if four:
                    ret_copies(s - 3, 4, 5)

            slots(act, slot)

        @block.vector
        def _(dve):
            def stats(N, src, i):
                for t in range(T):
                    ins = dve.bn_stats(N.st[:, t, :], src[:, t, :])
                ins.then_inc(N.stats, 1)
                dve.wait_ge(N.stats, i + 1)
                apart(dve, "dve")
                for t in range(T):
                    ins = dve.bn_aggr(N.mv[:, t, :], N.st[:, t, :])
                ins.then_inc(N.moments, 1)

            def apply(N, src, z, i, turned=None):
                dve.wait_ge(N.rdev, i + 1)
                if turned is not None:
                    dve.wait_ge(turned, i)
                for t in range(T):
                    ins = dve.tensor_scalar(z[:, t, :], src[:, t, :], N.mv[:, t, 0:1], N.rstd[:, t:t + 1], ALU.subtract, ALU.mult)
                ins.then_inc(N.done, 1)

            def prepare():
                dve.wait_ge(qk_in, 16 * 4)
                dve.wait_ge(biases_in, 16 * (NB - 2))
                dve.tensor_copy(browp[0:1, 0, :], brow[0:1, 0, :]).then_inc(bias_split, 1)
                for n in range(PARTS - 1):
                    dve.wait_ge(bias_split, 2 * n + 1)
                    dve.tensor_tensor(brow[0:1, n + 1, :], brow[0:1, n, :], browp[0:1, n, :], ALU.subtract).then_inc(bias_split, 1)
                    dve.wait_ge(bias_split, 2 * n + 2)
                    dve.tensor_copy(browp[0:1, n + 1, :], brow[0:1, n + 1, :]).then_inc(bias_split, 1)
                dve.wait_ge(masks_in, 16)
                dve.tensor_copy(cb[:, :], masks_f32[:, :]).then_inc(masks_ready, 1)

            def stats_a(i):
                dve.wait_ge(xin_in, 16 * (i + 1))
                stats(norm_a, x_in, i)

            def apply_a(i):
                apply(norm_a, x_in, zA, i, zAT_psum)
                if isinstance(i, int) and i == 0:
                    prepare()

            def rope_products(i):
                dve.wait_ge(qkA_psum, i + 1)
                dve.wait_ge(rotated, i)
                if isinstance(i, int) and i == 0:
                    dve.wait_ge(rope_in, 16)
                qk = psum["a_qk"][:, :].rearrange("p (w f e) -> p w f e", w=2 * T, e=2)
                for n in range(2):
                    src = qk[:, :, :, n].unsqueeze(2).to_broadcast([P, 2 * T, 2, D // 2])
                    dve.tensor_tensor(prod[:, n, :].rearrange("p (w c f) -> p w c f", w=2 * T, c=2), src,
                                      rope[:, n, :].rearrange("p (w c f) -> p w c f", w=2 * T, c=2), ALU.mult).then_inc(products, 1)

            def rest_a(i):
                dve.wait_ge(splitA, 3 * i + 1)
                dve.tensor_tensor(remA[:, :], psum["a_turn_qk"][:, :], partsA[:, 0, :], ALU.subtract).then_inc(splitA_rem, 1)

            def last_a(i):
                dve.wait_ge(splitA, 3 * i + 2)
                dve.wait_ge(splitA_rem, i + 1)
                dve.tensor_tensor(partsA[:, 2, :], remA[:, :], partsA[:, 1, :], ALU.subtract).then_inc(splitA, 1)

            def row_max(i, k):
                dve.wait_ge(scores_full, NFILL * i + k + 1)
                if k == 0:
                    dve.wait_ge(maxp_ready, 2 * i)
                t, h, n = SCORE_FILLS[k]
                dve.tensor_reduce(mx[:, t, h:h + n], ring[k % 2][:, :].rearrange("p (h k) -> p h k", h=n), AX_X, ALU.max).then_inc(scores_max, 1)

            def normalise(i):
                dve.wait_ge(oAT_psum, i + 1)
                whole = psum["o_turn"][:, :]
                sums = bass.AP(whole.tensor, whole.offset + HD, [whole.ap[0], [CT, T * H // 2], [SLOT, 2]])
                vals = bass.AP(whole.tensor, whole.offset, [whole.ap[0], [CT, T * H // 2], [SLOT, 2], [1, HD]])
                dve.reciprocal(rsum[:, :, :], sums).then_inc(rsum_ready, 1)
                dve.wait_ge(rsum_ready, i + 1)
                dve.wait_ge(ctxT_psum, i)
                dve.tensor_tensor(ctxA[:, :, :].rearrange("p t (g n d) -> p (t g) n d", n=2, d=HD), vals,
                                  rsum[:, :, :].unsqueeze(3).to_broadcast([P, T * H // 2, 2, HD]), ALU.mult).then_inc(ctx_ready, 1)

            def residual_a(i):
                dve.wait_ge(projA, i + 1)
                dve.wait_ge(xres_in, 16 * (i + 1))
                dve.wait_ge(f1.x_ready, i)
                dve.tensor_tensor(x1[:, :, :].rearrange("p t d -> p (t d)"), x_res[:, :, :].rearrange("p t d -> p (t d)"),
                                  psum["a_out"][:, S:2 * S], ALU.add).then_inc(x1_ready, 1)

            def ffn_mix(F, i):
                dve.wait_ge(F.zT_ready, i + 1)
                if F is f1 and isinstance(i, int) and i == 0:
                    dve.wait_ge(vecs_in, 16 * 7)
                now, before = F.zT[:, 1:1 + S], F.zT[:, 0:S]
                dve.tensor_tensor(F.dz[:, :], now, before, ALU.subtract).then_inc(F.dz_ready, 1)
                dve.wait_ge(F.dz_ready, i + 1)
                for n in range(2):
                    dve.scalar_tensor_tensor(out=F.mix[:, n, :], in0=F.dz[:, :], scalar=vecs[:, n:n + 1], in1=before,
                                             op0=ALU.mult, op1=ALU.add).then_inc(F.mixed, 1)

            def ffn_out(F, i, free):
                dve.wait_ge(F.v_ready, i + 1)
                dve.wait_ge(F.tanh_done, i + 1)
                flat = lambda v: v[:, :, :].rearrange("p t d -> p (t d)")
                dve.scalar_tensor_tensor(out=flat(F.u), in0=flat(F.th), scalar=1.0, in1=psum[F.name + "_v"][:, 0:S],
                                         op0=ALU.add, op1=ALU.mult).then_inc(F.gated, 1)
                dve.wait_ge(F.gated, i + 1)
                free(i)
                dve.scalar_tensor_tensor(out=flat(F.dst), in0=flat(F.u), scalar=0.5, in1=flat(F.src),
                                         op0=ALU.mult, op1=ALU.add).then_inc(F.x_ready, 1)

            def stats_f1(i):
                dve.wait_ge(x1_ready, i + 1)
                stats(norm_f1, x1, i)

            def stats_b(i):
                dve.wait_ge(f1.x_ready, i + 1)
                stats(norm_b, x2, i)

            def decay_qk(i):
                dve.wait_ge(qkB_psum, i + 1)
                dve.wait_ge(oB_psum, i)
                for n in range(2):
                    ins = dve.scalar_tensor_tensor(out=qkS[:, n, :], in0=psum["b_qk"][:, n * S:(n + 1) * S], scalar=vecs[:, 5 + n:6 + n],
                                                   in1=qk_decay[:, n * S:(n + 1) * S], op0=ALU.add, op1=ALU.mult)
                ins.then_inc(qkS_ready, 1)

            def rest_b(i):
                dve.wait_ge(splitB, 3 * i + 1)
                dve.tensor_tensor(remB[:, :], qkS[:, :, :].rearrange("p n s -> p (n s)"), partsB[:, 0, :], ALU.subtract).then_inc(splitB_rem, 1)

            def last_b(i):
                dve.wait_ge(splitB_rem, i + 1)
                dve.wait_ge(splitB, 3 * i + 2)
                dve.tensor_tensor(partsB[:, 2, :], remB[:, :], partsB[:, 1, :], ALU.subtract).then_inc(splitB, 1)

            def keep_heads(i):
                dve.wait_ge(kv_psum, i + 1)
                dve.wait_ge(oB_psum, i)
                dve.tensor_tensor(state[:, :], psum["b_kv"][:, D:2 * D], same_head, ALU.mult).then_inc(state_ready, 1)

            def r_values():
                return psum["b_turn_o"][:, 0:S].rearrange("p (t d) -> p t d", t=T)

            def stats_r(i):
                dve.wait_ge(oBT_psum, i + 1)
                stats(norm_r, r_values(), i)

            def gated_b(i):
                dve.wait_ge(nT_ready, i + 1)
                dve.wait_ge(gate_ready, i + 1)
                dve.wait_ge(projB, i)
                dve.scalar_tensor_tensor(out=yT[:, :], in0=gate[:, :], scalar=1.0, in1=nT[:, :], op0=ALU.add, op1=ALU.mult).then_inc(yT_ready, 1)

            def residual_b(i):
                dve.wait_ge(projB, i + 1)
                dve.wait_ge(x2_copied, 16 * (i + 1))
                dve.tensor_tensor(x3[:, :, :].rearrange("p t d -> p (t d)"), x2_res[:, :, :].rearrange("p t d -> p (t d)"),
                                  psum["b_out"][:, S:2 * S], ALU.add).then_inc(projB_used, 1)

            def stats_f2(i):
                dve.wait_ge(projB_used, i + 1)
                stats(norm_f2, x3, i)

            def x2_free(i):
                dve.wait_ge(x2_copied, 16 * i)

            def x4_free(i):
                dve.wait_ge(out_done, 16 * i)

            def row_maxima(i, first, last):
                for k in range(first, last):
                    row_max(i, k)

            def slot(s):
                one, two, three, four, five = (running(s, n) for n in range(5))
                if four:
                    stats_b(s - 3)
                    apply(norm_b, x2, zB, s - 3, zBT_psum)
                if five:
                    stats_r(s - 4)
                if one:
                    stats_a(s)
                if five:
                    apply(norm_r, r_values(), zR, s - 4, zRT_psum)
                if four:
                    decay_qk(s - 3)
                if one:
                    apply_a(s)
                if two:
                    row_maxima(s - 1, 0, 1)
                if five:
                    gated_b(s - 4)
                if four:
                    rest_b(s - 3)
                if two:
                    row_maxima(s - 1, 1, 2)
                if five:
                    residual_b(s - 4)
                if four:
                    last_b(s - 3)
                if two:
                    row_maxima(s - 1, 2, 3)
                if five:
                    stats_f2(s - 4)
                if two:
                    row_maxima(s - 1, 3, 4)
                if three:
                    normalise(s - 2)
                if five:
                    apply(norm_f2, x3, f2.z, s - 4)
                if two:
                    row_maxima(s - 1, 4, 6)
                if one:
                    rope_products(s)
                if five:
                    ffn_mix(f2, s - 4)
                if three:
                    residual_a(s - 2)
                    stats_f1(s - 2)
                if two:
                    row_maxima(s - 1, 6, 7)
                if four:
                    keep_heads(s - 3)
                if two:
                    row_maxima(s - 1, 7, 8)
                if three:
                    apply(norm_f1, x1, f1.z, s - 2)
                if two:
                    row_maxima(s - 1, 8, 10)
                if three:
                    ffn_mix(f1, s - 2)
                if one:
                    rest_a(s)
                if two:
                    row_maxima(s - 1, 10, 12)
                if one:
                    last_a(s)
                if five:
                    ffn_out(f2, s - 4, x4_free)
                if three:
                    ffn_out(f1, s - 2, x2_free)

            slots(dve, slot)

        @block.tensor
        def _(pe):
            def turn(dst, src, n=T):
                for t in range(n):
                    ins = pe.transpose(dst[:, t * P:(t + 1) * P], src[:, t, :], ident)
                return ins

            def first_bias(i):
                if isinstance(i, int) and i == 0:
                    pe.wait_ge(late_in, 16 * 7)
                    pe.wait_ge(bias_rows_in, 16 * PARTS)

            def add_bias(dst, first, width):
                return pe.matmul(dst, ones3[:, :], bias[:, first * D:first * D + width], start=False, stop=True, skip_group_check=True)

            read = {"a_turn": (zAT_ready, 1), "a_qk": (products, 2), "a_turn_qk": (splitA_rem, 1), "a_v": (vA_ready, 1),
                    "turn_max0": (maxT_ready, 2), "turn_max1": (maxT_ready, 2), "pv": (oA_ready, 1), "o_turn": (ctx_ready, 1),
                    "ctx_turn": (ctxT_ready, 1), "a_out": (x1_ready, 1),
                    "f1_turn": (f1.zT_ready, 1), "f1_rk": (f1.tanh_done, 1), "f1_v": (f1.gated, 1),
                    "b_turn": (zBT_ready, 1), "b_qk": (qkS_ready, 1), "b_vg": (gate_ready, 1), "turn_k": (kdec_ready, 1), "b_kv": (state_ready, 1),
                    "b_pv": (oB_ready, 1), "b_turn_o": (norm_r.done, 1), "b_turn_n": (nT_ready, 1), "b_out": (projB_used, 1),
                    "f2_turn": (f2.zT_ready, 1), "f2_rk": (f2.tanh_done, 1), "f2_v": (f2.gated, 1)}

            def bank_free(name, i):
                at = [n for n, _, _ in PSUM_USES].index(name)
                _, number, stage = PSUM_USES[at]
                for back in range(1, STAGES * len(PSUM_USES)):
                    prev, its, its_stage = PSUM_USES[(at - back) % len(PSUM_USES)]
                    if its != number:
                        continue
                    j = i + (stage - its_stage) + (at - back) // len(PSUM_USES)
                    if isinstance(j, int) and not 0 <= j < B:
                        continue
                    if prev.startswith("ret"):
                        return pe.wait_ge(ret_copied, NRET * j + int(prev[3:]) + 1)
                    signal, count = read[prev]
                    return pe.wait_ge(signal, count * j + (1 if prev == "turn_max0" else count))

            pe.wait_ge(ident_in, 16)

            def prepare():
                pe.wait_ge(wf_in, 16 * 3)
                for n in range(3):
                    ins = pe.transpose(ring[0][:, n * D:(n + 1) * D], wf[:, n, :], ident)
                ins.then_inc(wf_turned, 1)
                pe.wait_ge(wf_ready, 1)
                pe.wait_ge(cleared, 6)

            def a_turn(i):
                pe.wait_ge(norm_a.done, i + 1)
                bank_free("a_turn", i)
                turn(psum["a_turn"], zA).then_inc(zAT_psum, 1)

            def a_qk(i):
                pe.wait_ge(zAT_ready, i + 1)
                if isinstance(i, int) and i == 0:
                    pe.wait_ge(qk_in, 16 * 4)
                    pe.wait_ge(first_cleared, 4)
                bank_free("a_qk", i)
                for t in range(T):
                    dst = psum["a_qk"][:, t * QKW:(t + 1) * QKW]
                    pe.matmul(dst, zAT[:, t * P:(t + 1) * P], wa[:, 0:2, :].rearrange("p n d -> p (n d)"), start=True, stop=False, skip_group_check=True)
                    if isinstance(i, int) and i <= 1:
                        ins = pe.matmul(dst, ones1[:, :], brow[0:1, 0, 0:QKW], start=False, stop=True, skip_group_check=True)
                    else:
                        ins = add_bias(dst, 0, QKW)
                ins.then_inc(qkA_psum, 1)
                if isinstance(i, int) and i == 0:
                    prepare()

            def a_turn_qk(i):
                pe.wait_ge(rotated, i + 1)
                bank_free("a_turn_qk", i)
                for n in range(2):
                    for t in range(T):
                        ins = pe.transpose(psum["a_turn_qk"][:, n * S + t * P:n * S + (t + 1) * P], rot[:, t, n, :], ident)
                ins.then_inc(rotT_psum, 1)

            def a_v(i):
                pe.wait_ge(zAT_ready, i + 1)
                first_bias(i)
                bank_free("a_v", i)
                for t in range(T):
                    dst = psum["a_v"][:, t * D:(t + 1) * D]
                    pe.matmul(dst, zAT[:, t * P:(t + 1) * P], wa[:, 2, :], start=True, stop=False, skip_group_check=True)
                    ins = add_bias(dst, 2, D)
                ins.then_inc(vA_psum, 1)

            def score_fill(i, k):
                if k % 6 == 0:
                    pe.wait_ge(stackA_in[k // 6], 16 * NSTACK * (i + 1))
                if k >= 2:
                    pe.wait_ge(scores_max, NFILL * i + k - 1)
                else:
                    pe.wait_ge(scores_max, NFILL * i)
                if k == 0 and isinstance(i, int) and i == 0:
                    pe.wait_ge(masks_ready, 1)
                t, h0, heads = SCORE_FILLS[k]
                dst = ring[k % 2]
                if t == 0:
                    pe.matmul(dst[:, :], identb, future, start=True, stop=False, skip_group_check=True)
                else:
                    pe.matmul(dst[:, :].rearrange("p (h k) -> p h k", h=2)[:, :, P:S], identb,
                              future[:, 0:2 * P].rearrange("p (h k) -> p h k", h=2), start=True, stop=False, skip_group_check=True)
                w = (t + 1) * P
                for n in range(heads):
                    ins = pe.matmul(dst[:, n * w:(n + 1) * w], Qst[0:ROWS, h0 + n, t * P:(t + 1) * P], Kst[0:ROWS, h0 + n, 0:w],
                                    start=False, stop=True, skip_group_check=True)
                ins.then_inc(scores_full, 1)

            def scores(i, first, last):
                for k in range(first, last):
                    score_fill(i, k)

            def turn_max(i, half_):
                pe.wait_ge(maxp_ready, 2 * i + half_ + 1)
                bank_free(f"turn_max{half_}", i)
                apart(pe, "pe")
                dst = psum[f"turn_max{half_}"][0:PARTS * HALF, half_ * P:(half_ + 1) * P].bitcast(BF16)
                for t in range(T):
                    ins = pe.transpose(dst[:, t * P:(t + 1) * P], maxp[:, t, half_, :, :].rearrange("p n h -> p (n h)"), identb)
                ins.then_inc(maxT_psum, 1)

            def exp_fill(i, g):
                if g % 6 == 0:
                    pe.wait_ge(max_rows_in[g // 6], 16 * (i + 1))
                if g >= 2:
                    pe.wait_ge(exp_done, NFILL * i + g - 1)
                else:
                    pe.wait_ge(exp_done, NFILL * i)
                _, kt, h0 = EXP_FILLS[g]
                dst = exp_ring[g % 2]
                w = S if kt == 0 else P
                for n in range(512 // w):
                    h = h0 + n
                    ins = pe.matmul(dst[:, n * w:(n + 1) * w], Kst[0:XROWS, h, kt * P:(kt + 1) * P], Qst[0:XROWS, h, S - w:S], start=True, stop=True, skip_group_check=True)
                ins.then_inc(st_full, 1)

            def exp_fills(i, first, last):
                for g in range(first, last):
                    exp_fill(i, g)

            def pv(i, half_, kt):
                pe.wait_ge(masked, 2 * NMASK * i + NMASK * half_ + 2 * (kt + 1))
                if half_ == 0 and kt == 0:
                    pe.wait_ge(vA_ready, i + 1)
                    bank_free("pv", i)
                o = half_ * S
                for n in range(2):
                    for j in range(NCT):
                        h = hs(half_, j, n)
                        rhs = P0[:, h, :] if kt == 0 else P1[:, h, :]
                        ins = pe.matmul(psum["pv"][j * CT:(j + 1) * CT, o + kt * P:o + S], VA[:, kt, h, :], rhs,
                                        start=(half_ == 0 and kt == 0 and n == 0), stop=(kt == 1 and n == 1), skip_group_check=True)
                if kt == 1:
                    ins.then_inc(pv_done, 1)

            def o_turn(i):
                pe.wait_ge(oA_ready, i + 1)
                bank_free("o_turn", i)
                for t in range(T):
                    for half_ in range(2):
                        ins = pe.transpose(psum["o_turn"][:, (2 * t + half_) * P:(2 * t + half_ + 1) * P], oA[:, half_ * S + t * P:half_ * S + (t + 1) * P], ident)
                ins.then_inc(oAT_psum, 1)

            def ctx_turn(i):
                pe.wait_ge(ctx_ready, i + 1)
                bank_free("ctx_turn", i)
                turn(psum["ctx_turn"], ctxA).then_inc(ctxT_psum, 1)

            def a_out(i):
                pe.wait_ge(ctxT_ready, i + 1)
                bank_free("a_out", i)
                for t in range(T):
                    dst = psum["a_out"][:, S + t * D:S + (t + 1) * D]
                    pe.matmul(dst, ctxT[:, t * P:(t + 1) * P], wa[:, 3, :], start=True, stop=False, skip_group_check=True)
                    ins = add_bias(dst, 3, D)
                ins.then_inc(projA, 1)

            def ffn_turn(F, i):
                pe.wait_ge(F.norm.done, i + 1)
                bank_free(F.name + "_turn", i)
                turn(psum[F.name + "_turn"], F.z).then_inc(F.turned, 1)

            def ffn_rk(F, i):
                pe.wait_ge(F.mixed, 2 * (i + 1))
                bank_free(F.name + "_rk", i)
                for t in range(T):
                    pe.matmul(psum[F.name + "_rk"][:, S + t * D:S + (t + 1) * D], F.mix[:, 0, t * P:(t + 1) * P], wfT[:, 0, :], start=True, stop=True)
                pe.matmul(psum[F.name + "_rk"][:, 0:S], wfT[:, 1, :], F.mix[:, 1, :], start=True, stop=True).then_inc(F.rk_ready, 1)

            def ffn_v(F, i):
                pe.wait_ge(F.squared, i + 1)
                bank_free(F.name + "_v", i)
                for t in range(T):
                    ins = pe.matmul(psum[F.name + "_v"][:, t * D:(t + 1) * D], F.ka[:, t * P:(t + 1) * P], wfT[:, 2, :], start=True, stop=True)
                ins.then_inc(F.v_ready, 1)

            def b_turn(i):
                pe.wait_ge(norm_b.done, i + 1)
                bank_free("b_turn", i)
                turn(psum["b_turn"], zB).then_inc(zBT_psum, 1)

            def b_qk(i):
                pe.wait_ge(zBT_ready, i + 1)
                if isinstance(i, int) and i == 0:
                    pe.wait_ge(ordered, 2)
                bank_free("b_qk", i)
                for n in range(2):
                    ins = pe.matmul(psum["b_qk"][:, n * S:(n + 1) * S], wqk_dh[:, n, :], zBT[:, :], start=True, stop=True)
                ins.then_inc(qkB_psum, 1)

            def b_vg(i):
                pe.wait_ge(zBT_ready, i + 1)
                bank_free("b_vg", i)
                for t in range(T):
                    dst = psum["b_vg"][:, t * D:(t + 1) * D]
                    pe.matmul(dst, zBT[:, t * P:(t + 1) * P], wb[:, 2, :], start=True, stop=False, skip_group_check=True)
                    add_bias(dst, 4, D)
                pe.matmul(psum["b_vg"][:, S:2 * S], wb[:, 3, :], zBT[:, :], start=True, stop=True).then_inc(vg_psum, 1)

            def turn_k(i):
                bank_free("turn_k", i)
                pe.wait_ge(qkS_ready, i + 1)
                pe.transpose(psum["turn_k"][:, 0:D], qkS[:, 1, 0:P], ident).then_inc(kB_psum, 1)

            def b_kv(i):
                pe.wait_ge(kdec_ready, i + 1)
                pe.wait_ge(vB_ready, i + 1)
                bank_free("b_kv", i)
                first = quad_view(VB)[:, 0:NCT, :, :]
                pe.matmul(psum["b_kv"][:, D:2 * D], kdec[:, :], first, start=True, stop=True).then_inc(kv_psum, 1)

            def ret_fill(i, k):
                if k % 4 == 0:
                    pe.wait_ge(stackB_in[k // 4], 16 * NSTACK * (i + 1))
                bank_free(f"ret{k}", i)
                t, h0 = RET_FILLS[k]
                for n in range(4):
                    h = h0 + n
                    ins = pe.matmul(psum[f"ret{k}"][:, n * P:(n + 1) * P], Rk[:, h, t * P:(t + 1) * P], Rq[:, h, t * P:(t + 1) * P], start=True, stop=True, skip_group_check=True)
                ins.then_inc(ret_full, 1)

            def ret_fills(i, first, last):
                for k in range(first, last):
                    ret_fill(i, k)

            def b_pv(i, t):
                pe.wait_ge(ret_done, NRET * i + 6 + 2 * t)
                if t == 0:
                    bank_free("b_pv", i)
                if t == 1:
                    pe.wait_ge(state_ready, i + 1)
                    pe.matmul(psum["b_pv"][:, P:S], state[:, :], qkS[:, 0, P:S], start=False, stop=False, skip_group_check=True)
                for n in range(4):
                    for j in range(NCT):
                        h = 4 * j + n
                        ins = pe.matmul(psum["b_pv"][j * CT:(j + 1) * CT, t * P:(t + 1) * P], VB[:, t, h, :], PR[:, t, h, :],
                                        start=(t == 0 and n == 0), stop=(n == 3), skip_group_check=True)
                if t == 1:
                    ins.then_inc(oB_psum, 1)

            def b_turn_o(i):
                pe.wait_ge(oB_ready, i + 1)
                bank_free("b_turn_o", i)
                for t in range(T):
                    ins = pe.transpose(psum["b_turn_o"][:, t * P:(t + 1) * P], oB[:, t * P:(t + 1) * P], ident)
                ins.then_inc(oBT_psum, 1)

            def b_turn_n(i):
                pe.wait_ge(norm_r.done, i + 1)
                bank_free("b_turn_n", i)
                turn(psum["b_turn_n"], zR).then_inc(zRT_psum, 1)

            def b_out(i):
                pe.wait_ge(yT_ready, i + 1)
                bank_free("b_out", i)
                for t in range(T):
                    dst = psum["b_out"][:, S + t * D:S + (t + 1) * D]
                    pe.matmul(dst, yT[:, t * P:(t + 1) * P], wb[:, 4, :], start=True, stop=False, skip_group_check=True)
                    ins = add_bias(dst, 5, D)
                ins.then_inc(projB, 1)

            def slot(s):
                one, two, three, four, five = (running(s, n) for n in range(5))
                if three:
                    exp_fills(s - 2, 2, 3)
                if four:
                    ffn_v(f1, s - 3)
                if three:
                    exp_fills(s - 2, 3, 4)
                    turn_max(s - 2, 1)
                    exp_fills(s - 2, 4, 5)
                if five:
                    b_pv(s - 4, 1)
                if three:
                    exp_fills(s - 2, 5, 6)
                    pv(s - 2, 0, 0)
                if five:
                    b_turn_o(s - 4)
                if three:
                    exp_fills(s - 2, 6, 7)
                if four:
                    b_turn(s - 3)
                if three:
                    exp_fills(s - 2, 7, 8)
                    pv(s - 2, 0, 1)
                    exp_fills(s - 2, 8, 9)
                if four:
                    b_qk(s - 3)
                if three:
                    exp_fills(s - 2, 9, 11)
                if five:
                    b_turn_n(s - 4)
                if two:
                    scores(s - 1, 0, 2)
                if three:
                    exp_fills(s - 2, 11, 12)
                if one:
                    a_turn(s)
                if two:
                    scores(s - 1, 2, 3)
                if five:
                    b_out(s - 4)
                if three:
                    pv(s - 2, 1, 0)
                    pv(s - 2, 1, 1)
                if four:
                    turn_k(s - 3)
                if two:
                    scores(s - 1, 3, 4)
                    a_v(s - 1)
                    scores(s - 1, 4, 5)
                if three:
                    o_turn(s - 2)
                if four:
                    b_vg(s - 3)
                if two:
                    scores(s - 1, 5, 6)
                if one:
                    a_qk(s)
                if three:
                    ctx_turn(s - 2)
                if five:
                    ffn_turn(f2, s - 4)
                if four:
                    b_kv(s - 3)
                if two:
                    scores(s - 1, 6, 7)
                if three:
                    a_out(s - 2)
                if two:
                    scores(s - 1, 7, 8)
                    turn_max(s - 1, 0)
                if five:
                    ffn_rk(f2, s - 4)
                if four:
                    ret_fills(s - 3, 0, 2)
                if two:
                    scores(s - 1, 8, 9)
                if four:
                    ret_fills(s - 3, 2, 3)
                if two:
                    scores(s - 1, 9, 10)
                if three:
                    ffn_turn(f1, s - 2)
                if four:
                    ret_fills(s - 3, 3, 4)
                if one:
                    a_turn_qk(s)
                if two:
                    scores(s - 1, 10, 11)
                if four:
                    ret_fills(s - 3, 4, 7)
                if two:
                    exp_fills(s - 1, 0, 2)
                    scores(s - 1, 11, 12)
                if three:
                    ffn_rk(f1, s - 2)
                if four:
                    ret_fills(s - 3, 7, 8)
                if five:
                    ffn_v(f2, s - 4)
                if four:
                    b_pv(s - 3, 0)

            slots(pe, slot)


_OUT = ((B, S, D), "float32")
_A = ["Wq", "bq", "Wk", "bk", "Wv", "bv", "Wo", "bo"]
_B = ["Wq", "bq", "Wk", "bk", "Wv", "bv", "Wg", "bg", "Wo", "bo", "gamma", "beta"]
_F = ["W_r", "W_k", "W_v", "mu_r", "mu_k"]


def kernel(**inputs):
    import concourse.bacc as _bacc
    from concourse.bass_utils import run_bass_kernel_spmd as _run

    nc = _bacc.Bacc("TRN2", target_bir_lowering=False, num_devices=1)
    arrays = {}

    def given(name, value):
        v = np.ascontiguousarray(value)
        arrays[f"in_{name}"] = v
        return nc.dram_tensor(f"in_{name}", v.shape, mybir.dt.from_np(v.dtype), kind="ExternalInput").ap()

    x = given("x", inputs["L0_attn_a_x"])
    a = {n: given(f"a_{n}", inputs[f"L0_attn_a_{n}"]) for n in _A}
    b = {n: given(f"b_{n}", inputs[f"L0_attn_b_{n}"]) for n in _B}
    f = {n: given(f"f_{n}", inputs[f"L0_ffn_{n}"]) for n in _F}
    c = {n: given(n, v) for n, v in constants().items()}
    out = nc.dram_tensor("out", _OUT[0], mybir.dt.from_np(np.dtype(_OUT[1])), kind="ExternalOutput").ap()
    build(nc, x, a, b, f, c, out)
    r = _run(nc, [arrays], core_ids=[0])
    return r.results[0]["out"]
```
